# Optimizing a Trainium2 kernel written in Bass

```python
import numpy as np
import jax
import jax.numpy as jnp

def _softmax(x, axis=-1):
    return jax.nn.softmax(x, axis=axis)

def _gelu(x):
    return jax.nn.gelu(x, approximate=True)

def _silu(x):
    return jax.nn.silu(x)

def _sigmoid(x):
    return jax.nn.sigmoid(x)

def _layernorm(x, axis=-1, eps=1e-05):
    m = jnp.mean(x, axis=axis, keepdims=True)
    v = jnp.var(x, axis=axis, keepdims=True)
    return (x - m) / jnp.sqrt(v + eps)

def _scatter_add(tgt, idx, src, axis=0):
    return tgt.at[idx].add(src)

def _segment_sum(src, seg, n):
    return jax.ops.segment_sum(src, seg, n)
kernel_name = 'mk_adj_preln_d2_adj_r2_984c3d'

def setup_inputs(seed: int=0):
    np.random.seed(seed)
    _w = jnp.asarray

    def _rec_inputs():
        import jax
        import jax.numpy as jnp
        _gk = jax.random.key(seed)
        x = -0.0003929 + 0.9999 * jax.random.normal(jax.random.fold_in(_gk, 1), (32, 256, 128), jnp.float32)
        _a = jax.random.bernoulli(jax.random.fold_in(_gk, 2), 0.03125, (256, 256))
        _a = jnp.logical_or(_a, jnp.swapaxes(_a, -1, -2))
        _a = jnp.logical_or(_a, jnp.eye(256, dtype=bool))
        _af = _a.astype(jnp.float32)
        _af = _af * jax.random.uniform(jax.random.fold_in(_gk, 3), (256, 256), jnp.float32, 0.05, 1)
        adj = _af
        return (x, adj)
    x, adj = _rec_inputs()

    def _L0_gnn_setup():
        import jax, jax.numpy as jnp
        import numpy as np
        EPS = 1e-05

        def _batchnorm(x, gamma, beta):
            mu = jnp.mean(x, axis=0)
            var = jnp.var(x, axis=0)
            return (x - mu) * jax.lax.rsqrt(var + EPS) * gamma + beta
        key = jax.random.key(seed)
        ks = jax.random.split(key, 4)
        b, n, d, h, o = (32, 1024, 128, 256, 128)
        features = jax.random.normal(ks[0], (b, n, d), dtype=jnp.float32)
        A = jax.random.uniform(ks[1], (n, n), dtype=jnp.float32)
        lim1 = float(np.sqrt(6.0 / (d + h)))
        W1 = jax.random.uniform(ks[2], (h, d), minval=-lim1, maxval=lim1, dtype=jnp.float32)
        b1 = jnp.zeros((h,), jnp.float32)
        lim2 = float(np.sqrt(6.0 / (h + o)))
        W2 = jax.random.uniform(ks[3], (o, h), minval=-lim2, maxval=lim2, dtype=jnp.float32)
        b2 = jnp.zeros((o,), jnp.float32)
        g1 = jnp.ones((h,), jnp.float32)
        be1 = jnp.zeros((h,), jnp.float32)
        g2 = jnp.ones((o,), jnp.float32)
        be2 = jnp.zeros((o,), jnp.float32)
        return {'features': features, 'A': A, 'W1': W1, 'b1': b1, 'g1': g1, 'be1': be1, 'W2': W2, 'b2': b2, 'g2': g2, 'be2': be2}
    _L0_gnn_all = _L0_gnn_setup()
    _L0_gnn_in = {k: v for k, v in _L0_gnn_all.items() if k in ('W1', 'b1', 'g1', 'be1', 'W2', 'b2', 'g2', 'be2')}
    del _L0_gnn_all

    def _L1_gnn_setup():
        import jax, jax.numpy as jnp
        import numpy as np
        B, T, D, H = (64, 1024, 128, 128)
        MAX_SKIP = 4

        def _lstm_last(Wih, Whh, bih, bhh, xs):
            N, _, Hd = xs.shape
            bias = bih + bhh

            def step(carry, x_t):
                h, c = carry
                g = x_t @ Wih.T + h @ Whh.T + bias
                i, f, gg, o = jnp.split(g, 4, axis=-1)
                c = jax.nn.sigmoid(f) * c + jax.nn.sigmoid(i) * jnp.tanh(gg)
                h = jax.nn.sigmoid(o) * jnp.tanh(c)
                return ((h, c), None)
            init = (jnp.zeros((N, Hd), xs.dtype), jnp.zeros((N, Hd), xs.dtype))
            (h_last, _), _ = jax.lax.scan(step, init, jnp.swapaxes(xs, 0, 1))
            return h_last
        key = jax.random.key(seed)
        ks = jax.random.split(key, 8)
        s = 0.05
        x = jax.random.normal(ks[0], (B, T, D), jnp.float32)
        adj = jax.random.uniform(ks[1], (T, T), jnp.float32) / T
        Wg0 = jax.random.normal(ks[2], (D, H), jnp.float32) * s
        bg0 = jnp.zeros((H,), jnp.float32)
        Wg1 = jax.random.normal(ks[3], (H, H), jnp.float32) * s
        bg1 = jnp.zeros((H,), jnp.float32)
        Wih = jax.random.normal(ks[4], (MAX_SKIP, 4 * H, H), jnp.float32) * s
        Whh = jax.random.normal(ks[5], (MAX_SKIP, 4 * H, H), jnp.float32) * s
        bih = jax.random.normal(ks[6], (MAX_SKIP, 4 * H), jnp.float32) * s
        bhh = jax.random.normal(ks[7], (MAX_SKIP, 4 * H), jnp.float32) * s
        return dict(x=x, adj=adj, Wg0=Wg0, bg0=bg0, Wg1=Wg1, bg1=bg1, Wih=Wih, Whh=Whh, bih=bih, bhh=bhh)
    _L1_gnn_all = _L1_gnn_setup()
    _L1_gnn_in = {k: v for k, v in _L1_gnn_all.items() if k in ('Wg0', 'bg0', 'Wg1', 'bg1', 'Wih', 'Whh', 'bih', 'bhh')}
    del _L1_gnn_all
    return {'x': x, 'adj': adj, 'L0_gnn_W1': _L0_gnn_in['W1'], 'L0_gnn_b1': _L0_gnn_in['b1'], 'L0_gnn_g1': _L0_gnn_in['g1'], 'L0_gnn_be1': _L0_gnn_in['be1'], 'L0_gnn_W2': _L0_gnn_in['W2'], 'L0_gnn_b2': _L0_gnn_in['b2'], 'L0_gnn_g2': _L0_gnn_in['g2'], 'L0_gnn_be2': _L0_gnn_in['be2'], 'L1_gnn_Wg0': _L1_gnn_in['Wg0'], 'L1_gnn_bg0': _L1_gnn_in['bg0'], 'L1_gnn_Wg1': _L1_gnn_in['Wg1'], 'L1_gnn_bg1': _L1_gnn_in['bg1'], 'L1_gnn_Wih': _L1_gnn_in['Wih'], 'L1_gnn_Whh': _L1_gnn_in['Whh'], 'L1_gnn_bih': _L1_gnn_in['bih'], 'L1_gnn_bhh': _L1_gnn_in['bhh']}

def reference(x, adj, L0_gnn_W1, L0_gnn_b1, L0_gnn_g1, L0_gnn_be1, L0_gnn_W2, L0_gnn_b2, L0_gnn_g2, L0_gnn_be2, L1_gnn_Wg0, L1_gnn_bg0, L1_gnn_Wg1, L1_gnn_bg1, L1_gnn_Wih, L1_gnn_Whh, L1_gnn_bih, L1_gnn_bhh):
    import jax
    import jax.numpy as jnp

    def _L0_gnn_ref(features, A, W1, b1, g1, be1, W2, b2, g2, be2):
        import jax, jax.numpy as jnp
        import numpy as np
        EPS = 1e-05

        def _batchnorm(x, gamma, beta):
            mu = jnp.mean(x, axis=0)
            var = jnp.var(x, axis=0)
            return (x - mu) * jax.lax.rsqrt(var + EPS) * gamma + beta
        b, n, d = features.shape
        A_norm = A + jnp.eye(n, dtype=A.dtype)
        deg = jnp.sum(A_norm, axis=0) + jnp.sum(A_norm, axis=1) - jnp.diagonal(A_norm)
        dinv = jax.lax.rsqrt(deg)
        A_hat = A_norm * dinv[:, None] * dinv[None, :]
        agg = jnp.einsum('nm,bmd->bnd', A_hat, features)
        x = agg.reshape(-1, d)
        h = jax.nn.relu(_batchnorm(x @ W1.T + b1, g1, be1))
        out = h @ W2.T + b2
        out = _batchnorm(out, g2, be2)
        return out.reshape(b, n, -1)

    def _L1_gnn_ref(x, adj, Wg0, bg0, Wg1, bg1, Wih, Whh, bih, bhh):
        import jax, jax.numpy as jnp
        import numpy as np
        B, T, D, H = (64, 1024, 128, 128)
        MAX_SKIP = 4

        def _lstm_last(Wih, Whh, bih, bhh, xs):
            N, _, Hd = xs.shape
            bias = bih + bhh

            def step(carry, x_t):
                h, c = carry
                g = x_t @ Wih.T + h @ Whh.T + bias
                i, f, gg, o = jnp.split(g, 4, axis=-1)
                c = jax.nn.sigmoid(f) * c + jax.nn.sigmoid(i) * jnp.tanh(gg)
                h = jax.nn.sigmoid(o) * jnp.tanh(c)
                return ((h, c), None)
            init = (jnp.zeros((N, Hd), xs.dtype), jnp.zeros((N, Hd), xs.dtype))
            (h_last, _), _ = jax.lax.scan(step, init, jnp.swapaxes(xs, 0, 1))
            return h_last
        h = jax.nn.relu(jnp.einsum('ts,bsh->bth', adj, x @ Wg0 + bg0))
        h = jax.nn.relu(jnp.einsum('ts,bsh->bth', adj, h @ Wg1 + bg1))
        Bv, Tv, Hd = h.shape
        for p in range(1, MAX_SKIP + 1):
            nw = Tv // p
            wins = h[:, :nw * p, :].reshape(Bv * nw, p, Hd)
            last = _lstm_last(Wih[p - 1], Whh[p - 1], bih[p - 1], bhh[p - 1], wins)
            idx = jnp.arange(nw) * p + (p - 1)
            h = h.at[:, idx, :].set(last.reshape(Bv, nw, Hd))
        return h
    h = jnp.maximum(_layernorm(x, axis=-1), 0.0)
    x = x + _L0_gnn_ref(h, adj, L0_gnn_W1, L0_gnn_b1, L0_gnn_g1, L0_gnn_be1, L0_gnn_W2, L0_gnn_b2, L0_gnn_g2, L0_gnn_be2)
    h = jnp.maximum(_layernorm(x, axis=-1), 0.0)
    x = x + _L1_gnn_ref(h, adj, L1_gnn_Wg0, L1_gnn_bg0, L1_gnn_Wg1, L1_gnn_bg1, L1_gnn_Wih, L1_gnn_Whh, L1_gnn_bih, L1_gnn_bhh)
    return x

_drawn_inputs = setup_inputs


def setup_inputs(seed=0):
    import zlib

    import numpy as np

    out = dict(_drawn_inputs(seed))
    spreads = {'L0_gnn_b1': (0.0, 0.8),
     'L0_gnn_g1': (1.0, 0.2),
     'L0_gnn_be1': (0.0, 0.1),
     'L0_gnn_b2': (0.0, 0.8),
     'L0_gnn_g2': (1.0, 0.2),
     'L0_gnn_be2': (0.0, 0.1),
     'L1_gnn_bg0': (0.0, 0.1),
     'L1_gnn_bg1': (0.0, 0.381)}
    factors = {'L1_gnn_Whh': 8.0, 'L1_gnn_bih': 4.329, 'L1_gnn_bhh': 4.322}
    for name, (base, spread) in spreads.items():
        noise = np.random.default_rng([zlib.crc32(name.encode()), seed]).standard_normal(out[name].shape)
        drawn = base * np.exp(spread * noise) if base else spread * noise
        out[name] = jnp.asarray(drawn.astype(out[name].dtype))
    for name, factor in factors.items():
        out[name] = (out[name] * factor).astype(out[name].dtype)
    return out
```

```python
import concourse.bass as bass
from concourse import mybir
from contextlib import ExitStack

F32 = mybir.dt.float32
F32R = mybir.dt.float32r
ALU = mybir.AluOpType
ACT = mybir.ActivationFunctionType
AX = mybir.AxisListType

P = 128
KIB = 1024


def gnn_lstm_kernel(nc, x, adj, W1, b1, g1, be1, W2, b2, g2, be2,
                    Wg0, bg0, Wg1, bg1, Wih, Whh, bih, bhh, out):
    B, N, D = x.shape
    TT = N // P
    HH = W1.shape[0] // P
    GB = 4
    NG = B // GB
    GC = GB * N
    BANK = 512
    CHUNKS = NG // 2
    CB = 2 * GB
    CG = TT * CB
    SKIP = Wih.shape[0]
    GATES = Wih.shape[1] // P
    EPS = 1e-5
    R_B1, R_G1, R_BE1 = 0, HH, 2 * HH
    R_B2, R_G2, R_BE2 = 3 * HH, 3 * HH + 1, 3 * HH + 2
    R_BIH = 3 * HH + 3
    R_BHH = R_BIH + SKIP * GATES
    ROWS = R_BHH + SKIP * GATES

    ctx = ExitStack()
    with ctx:
        base = -(-nc.sbuf_base // 64) * 64

        def at(name, shape, dt, offset):
            return nc.alloc_sbuf_tensor_at(name, shape, dt, offset=base + offset)

        def np_prod(dims):
            n = 1
            for d in dims:
                n *= d
            return n

        AT_X, AT_Z, AT_Z2, AT_SCR, AT_WL, AT_SMALL = (k * KIB for k in (0, 32, 96, 128, 160, 188))
        x_row = at("x_row", [P, TT, B, D], F32, AT_X)
        z1 = at("z1", [P, HH, NG, GC], F32, AT_Z)
        h_hi = at("h_hi", [P, NG, GC], F32R, AT_Z)
        h_lo = at("h_lo", [P, NG, GC], F32R, AT_Z + 32 * KIB)
        z2 = at("z2", [P, NG, GC], F32, AT_Z2)
        agg_hi = at("agg_hi", [P, 2, GC], F32R, AT_Z2)
        agg_lo = at("agg_lo", [P, 2, GC], F32R, AT_Z2 + 8 * KIB)
        r_hi = at("r_hi", [P, 2, GC], F32R, AT_Z2 + 16 * KIB)
        r_lo = at("r_lo", [P, 2, GC], F32R, AT_Z2 + 24 * KIB)
        mid_hi = at("mid_hi", [P, 4, BANK], F32R, AT_Z2)
        mid_lo = at("mid_lo", [P, 4, BANK], F32R, AT_Z2 + 8 * KIB)
        cell = at("cell", [P, 4, BANK], F32, AT_Z2 + 16 * KIB)
        normed = at("normed", [P, 2, TT, GB, D], F32, AT_SCR)
        y_col = at("y_col", [P, 2, GC], F32, AT_SCR + 8 * KIB)
        raw_l = at("raw_l", [P, 2 * SKIP - 1, GATES, D], F32, AT_SCR + 8 * KIB)
        raw_a = at("raw_a", [P, TT, N], F32, AT_SCR + 22 * KIB)
        raw_1 = at("raw_1", [P, HH, D], F32, AT_SCR + 24 * KIB)
        raw_2 = at("raw_2", [P, HH * P], F32, AT_SCR + 25 * KIB)
        raw_g = at("raw_g", [P, 2, D], F32, AT_SCR + 26 * KIB)
        raw_bg = at("raw_bg", [P, 2, D], F32, AT_SCR + 27 * KIB)
        raw_v = at("raw_v", [ROWS, D], F32, AT_SCR + 28 * KIB)
        a_norm = at("a_norm", [P, TT, N], F32, AT_SCR + 29 * KIB)
        gate = at("gate", [P, 2, GATES, BANK], F32, AT_SCR)
        h_sum = at("h_sum", [P, 2, GC], F32, AT_SCR + 16 * KIB)
        o_row = at("o_row", [P, 2, TT, GB, D], F32, AT_SCR + 24 * KIB)
        small = {"at": AT_SMALL}

        def sb(name, shape, dt=F32):
            t = at(name, shape, dt, small["at"])
            small["at"] += -(-4 * np_prod(shape[1:]) // 32) * 32
            return t

        NMAT = 2 * SKIP - 1
        wl_hi = at("wl_hi", [P, NMAT, GATES, P], F32R, AT_WL)
        wl_lo = at("wl_lo", [P, NMAT, GATES, P], F32R, AT_WL + NMAT * 2 * KIB)
        ident = sb("ident", [P, P])
        ones = at("ones", [P, P], F32, AT_Z2 + 16 * KIB)
        adj_t = sb("adj_t", [P, TT, N])
        adj_hi = sb("adj_hi", [P, TT, N], F32R)
        adj_lo = sb("adj_lo", [P, TT, N], F32R)
        ahat_t = at("ahat_t", [P, TT, N], F32, AT_Z2 + 20 * KIB)
        w1_hi = at("w1_hi", [P, HH, P], F32R, AT_Z2 + 22 * KIB)
        w1_lo = at("w1_lo", [P, HH, P], F32R, AT_Z2 + 23 * KIB)
        w2_t = sb("w2_t", [P, HH, P])
        wg_hi = sb("wg_hi", [P, 2, P], F32R)
        wg_lo = sb("wg_lo", [P, 2, P], F32R)
        bg_r = sb("bg_r", [P, 2, P], F32R)
        bg_l = at("bg_l", [P, 2, P], F32R, AT_Z2 + 19 * KIB)
        rs_r = at("rs_r", [P, N], F32R, AT_Z2 + 17 * KIB)
        rs_l = at("rs_l", [P, N], F32R, AT_Z2 + 18 * KIB)
        rs_rows = sb("rs_rows", [P, 2, N], F32R)
        vec = sb("vec", [P, ROWS])
        lbias = sb("lbias", [P, SKIP * GATES])
        st1 = sb("st1", [P, HH, 2 * NG, 6])
        st2 = sb("st2", [P, 2 * NG, 6])
        mv = sb("mv", [P, 3, 2])
        sc_a = sb("sc_a", [P, 3])
        sh_a = sb("sh_a", [P, 3])
        tmp = sb("tmp", [P, 8, CG])
        lnst = sb("lnst", [P, CG, 6])
        rstd = sb("rstd", [P, CHUNKS, CG])
        shift = sb("shift", [P, CHUNKS, CG])
        deg = sb("deg", [P, 4, TT])
        ps = ctx.enter_context(nc.psum_tensor("ps", [P, 8, BANK], F32))

        def banks(first, count=2):
            return ps[:, first:first + count, :]

        def sem(name):
            return ctx.enter_context(nc.semaphore(name))

        ld_adj, ld_w, ld_vec, ld_bg, ld_lstm = (sem(n) for n in ("ld_adj", "ld_w", "ld_vec", "ld_bg", "ld_lstm"))
        ld_x = [sem(f"ld_x{c}") for c in range(CHUNKS)]
        x_landed = sem("x_landed")
        const_ready = sem("const_ready")
        setup_ps = sem("setup_ps")
        setup_sb = sem("setup_sb")
        wl_ps, wl_head, wl_done = sem("wl_ps"), sem("wl_head"), sem("wl_done")
        step = sem("step")
        var_ready, sd_ready = sem("var_ready"), sem("sd_ready")
        stat_ready = sem("stat_ready")
        normed_ready, agg_ps, agg_head, agg_tail = (sem(n) for n in ("normed_ready", "agg_ps", "agg_head", "agg_tail"))
        z1_ps, z1_sb = sem("z1_ps"), sem("z1_sb")
        bn1_ready, bn2_ready = sem("bn1_ready"), sem("bn2_ready")
        hid_ready, z2_ps, z2_sb = sem("hid_ready"), sem("z2_ps"), sem("z2_sb")
        y_ready, y_ps, x1_ready = sem("y_ready"), sem("y_ps"), sem("x1_ready")
        stat2_ready = sem("stat2_ready")
        normed2_ready, agg2_ps, agg2_head, agg2_tail = (sem(n) for n in ("normed2_ready", "agg2_ps", "agg2_head", "agg2_tail"))
        r_ps, r_head, r_tail = sem("r_ps"), sem("r_head"), sem("r_tail")
        u_ps, u_head, u_tail = sem("u_ps"), sem("u_head"), sem("u_tail")
        h_ps, h_head, h_tail = sem("h_ps"), sem("h_head"), sem("h_tail")
        gates_ps = sem("gates_ps")
        ig_ready, f_ready, o_ready = sem("ig_ready"), sem("f_ready"), sem("o_ready")
        c_ready, tc_ready, h_done = sem("c_ready"), sem("tc_ready"), sem("h_done")
        sum_ready, out_ps, row_ready = sem("sum_ready"), sem("out_ps"), sem("row_ready")
        out_done = [sem(f"out_done{k}") for k in range(2)]

        STEPS = []
        for w in range(1, SKIP + 1):
            count = N // w
            parts = -(-count * GB // BANK)
            for s in range(w):
                for c in range(parts):
                    STEPS.append((w, s, c * (count // parts), count // parts))
        HALF = NG // 2
        UNITS = len(STEPS) * HALF
        CARRY = sum(s > 0 for _, s, _, _ in STEPS) * HALF

        def seq(t, g, w, s, first, count):
            v = t[:, g, :].rearrange("p (t b) -> p t b", b=GB)
            lo = first * w + s
            return v[:, lo:lo + (count - 1) * w + 1:w, :]

        def steps_of_pair(half, j, n):
            unit = half * UNITS + (n * HALF + 2 * j)
            before = sum(s > 0 for _, s, _, _ in STEPS[:n])
            return unit, half * CARRY + (before * HALF + 2 * j)

        block = ctx.enter_context(nc.Block())

        @block.sync
        def _(sp):
            sp.dma_start(raw_a[:, :, :], adj.rearrange("(t p) m -> p t m", p=P)).then_inc(ld_adj, 16)
            for c in range(CHUNKS):
                for t in range(TT):
                    sp.dma_start(x_row[:, t, c * CB:(c + 1) * CB, :],
                                 x[c * CB:(c + 1) * CB, t * P:(t + 1) * P, :].rearrange("b p d -> p b d")
                                 ).then_inc(ld_x[c], 16)
            for w in range(SKIP):
                sp.dma_start(raw_l[:, w, :, :], Wih[w].rearrange("(q p) d -> p q d", p=P)).then_inc(ld_lstm, 16)
            for w in range(1, SKIP):
                sp.dma_start(raw_l[:, SKIP + w - 1, :, :], Whh[w].rearrange("(q p) d -> p q d", p=P)).then_inc(ld_lstm, 16)
            for c in range(CHUNKS):
                sp.wait_ge(ld_x[c], 16 * TT)
                sp.sem_inc(x_landed, 1)
            for k in range(2):
                sp.sem_inc(out_done[k], 16 * TT)
            with sp.Fori(0, CHUNKS) as i:
                for k in range(2):
                    sp.wait_ge(row_ready, 2 + 2 * i + k + 1)
                    for t in range(TT):
                        sp.dma_start(out[bass.ds(i * CB + k * GB, GB), t * P:(t + 1) * P, :].rearrange("b p d -> p b d"),
                                     o_row[:, k, t, :, :]).then_inc(out_done[k], 16)
            for k in range(2):
                sp.wait_ge(out_done[k], 16 * TT * (CHUNKS + 1))

        @block.gpsimd
        def _(pool):
            pool.dma_start(raw_1[:, :, :], W1.rearrange("(k p) d -> p k d", p=P)).then_inc(ld_w, 16)
            pool.dma_start(raw_2[:, :], W2).then_inc(ld_w, 16)
            pool.dma_start(raw_g[:, 0, :], Wg0).then_inc(ld_w, 16)
            pool.dma_start(raw_g[:, 1, :], Wg1).then_inc(ld_w, 16)
            for row, v in ((R_B1, b1), (R_G1, g1), (R_BE1, be1)):
                pool.dma_start(raw_v[row:row + HH, :], v.rearrange("(k p) -> k p", p=P)).then_inc(ld_vec, 16)
            for row, v in ((R_B2, b2), (R_G2, g2), (R_BE2, be2)):
                pool.dma_start(raw_v[row:row + 1, :], v.rearrange("(k p) -> k p", p=P)).then_inc(ld_vec, 16)
            for row, v in ((R_BIH, bih), (R_BHH, bhh)):
                pool.dma_start(raw_v[row:row + SKIP * GATES, :], v.rearrange("w (q p) -> (w q) p", p=P)).then_inc(ld_vec, 16)
            pool.memset(ident[:, :], 0.0).then_inc(const_ready, 1)
            pool.wait_ge(const_ready, 1)
            pool.affine_select(out=ident[:, :], in_=ident[:, :], compare_op=ALU.not_equal, fill=1.0,
                               base=0, pattern=[[-1, P]], channel_multiplier=1).then_inc(const_ready, 1)
            pool.memset(ones[:, :], 1.0).then_inc(const_ready, 1)
            pool.memset(rs_rows[:, :, :].bitcast(F32), 0.0).then_inc(const_ready, 1)
            pool.memset(raw_bg[:, :, :], 0.0).then_inc(const_ready, 1)
            pool.wait_ge(const_ready, 5)
            for q in (0, 32, 64):
                for layer, v in ((0, bg0), (1, bg1)):
                    pool.dma_start(raw_bg[q:q + 1, layer, :], v.rearrange("(k p) -> k p", p=P)).then_inc(ld_bg, 16)
            with pool.Fori(0, 2) as half:
                with pool.Fori(0, 2) as j:
                    for k in range(2):
                        unit, _ = steps_of_pair(half, j, len(STEPS) - 1)
                        pool.wait_ge(h_done, 2 + unit + k + 1)
                        pool.wait_ge(out_ps, half * HALF + 2 * j + k + 1)
                        g = half * HALF + 2 * j + k
                        pool.tensor_tensor(h_sum[:, k, :].rearrange("p (b t) -> p b t", b=GB),
                                           h_hi[:, g, :].bitcast(F32).rearrange("p (t b) -> p b t", b=GB),
                                           h_lo[:, g, :].bitcast(F32).rearrange("p (t b) -> p b t", b=GB),
                                           ALU.add).then_inc(sum_ready, 1)

        @block.tensor
        def _(pe):
            def three(dst, w_hi, w_lo, m_hi, m_lo, start, stop):
                pe.matmul(dst, w_hi, m_hi, start=start, stop=False, skip_group_check=True)
                pe.matmul(dst, w_hi, m_lo, start=False, stop=False, skip_group_check=True)
                return pe.matmul(dst, w_lo, m_hi, start=False, stop=stop, skip_group_check=True)

            pe.sem_inc(y_ps, 2)
            pe.sem_inc(out_ps, 2)
            pe.wait_ge(const_ready, 5)
            pe.wait_ge(ld_adj, 16)
            for m in range(TT):
                for n in range(TT):
                    last = pe.transpose(ps[:, 0, m * N + n * P:m * N + (n + 1) * P],
                                        raw_a[:, n, m * P:(m + 1) * P], ident[:, :])
            last.then_inc(setup_ps, 1)
            pe.wait_ge(ld_w, 64)
            for k in range(HH):
                pe.transpose(ps[:, 1, k * P:(k + 1) * P], raw_1[:, k, :], ident[:, :])
                last = pe.transpose(ps[:, 1, (HH + k) * P:(HH + k + 1) * P], raw_2[:, k * P:(k + 1) * P], ident[:, :])
            last.then_inc(setup_ps, 1)
            pe.wait_ge(ld_vec, 16 * 8)
            pe.transpose(ps[:, 2, 0:ROWS], raw_v[:, :], ident[0:ROWS, 0:ROWS]).then_inc(setup_ps, 1)
            pe.wait_ge(setup_sb, 1)
            for m in range(TT):
                last = pe.matmul(ps[:, 3, 0:N], ones[:, :], adj_t[:, m, :], start=m == 0, stop=m == TT - 1)
            last.then_inc(setup_ps, 1)
            pe.wait_ge(setup_sb, 2)
            for m in range(TT):
                for n in range(TT):
                    last = pe.transpose(ps[:, 4, m * N + n * P:m * N + (n + 1) * P],
                                        a_norm[:, n, m * P:(m + 1) * P], ident[:, :])
            last.then_inc(setup_ps, 1)
            pe.wait_ge(setup_sb, 3)

            with pe.Fori(0, CHUNKS) as i:
                for k in range(2):
                    pe.wait_ge(normed_ready, 2 * i + k + 1)
                    pe.wait_ge(agg_tail, 2 * i + k + 1)
                    for b in range(GB):
                        for m in range(TT):
                            last = pe.matmul(ps[:, 2 * k + b // 2, (b % 2) * N:(b % 2 + 1) * N],
                                             normed[:, k, m, b, :], ahat_t[:, m, :], start=m == 0, stop=m == TT - 1)
                    last.then_inc(agg_ps, 1)
                for k in range(2):
                    pe.wait_ge(agg_tail, 2 + 2 * i + k + 1)
                    for hh in range(HH):
                        pe.wait_ge(z1_sb, 2 * (2 * i + k) + hh + 1)
                        for c in range(2):
                            cols = slice(c * BANK, (c + 1) * BANK)
                            last = three(ps[:, 4 + 2 * hh + c, :], w1_hi[:, hh, :], w1_lo[:, hh, :],
                                         agg_hi[:, k, cols], agg_lo[:, k, cols], True, True)
                        last.then_inc(z1_ps, 1)

            pe.wait_ge(ld_lstm, 16 * NMAT)
            for n in range(NMAT):
                if n >= 4:
                    pe.wait_ge(wl_done, n - 3)
                for q in range(GATES):
                    last = pe.transpose(ps[:, n % 4, q * P:(q + 1) * P], raw_l[:, n, q, :], ident[:, :])
                last.then_inc(wl_ps, 1)

            with pe.Fori(0, CHUNKS) as i:
                for k in range(2):
                    pe.wait_ge(hid_ready, 2 * i + k + 1)
                    pe.wait_ge(z2_sb, 2 * i + k + 1)
                    for c in range(2):
                        for hh in range(HH):
                            last = pe.matmul(ps[:, 4 + 2 * k + c, :], w2_t[:, hh, :],
                                             z1[:, hh, 2 * i + k, c * BANK:(c + 1) * BANK],
                                             start=hh == 0, stop=hh == HH - 1)
                    last.then_inc(z2_ps, 1)

            with pe.Fori(0, CHUNKS) as i:
                for k in range(2):
                    pe.wait_ge(y_ready, 2 * i + k + 1)
                    pe.wait_ge(x1_ready, 2 * i + k + 1)
                    for t in range(TT):
                        for b in range(GB):
                            last = pe.transpose(ps[:, 4 + 2 * k + t, b * D:(b + 1) * D],
                                                y_col[:, k, b * N + t * P:b * N + (t + 1) * P], ident[:, :])
                    last.then_inc(y_ps, 1)

            pe.wait_ge(x1_ready, 2 + NG)
            with pe.Fori(0, CHUNKS) as i:
                for k in range(2):
                    pe.wait_ge(normed2_ready, 2 * i + k + 1)
                    pe.wait_ge(u_tail, 2 * i + k + 1)
                    for b in range(GB):
                        for m in range(TT):
                            last = pe.matmul(ps[:, 2 * k + b // 2, (b % 2) * N:(b % 2 + 1) * N],
                                             normed[:, k, m, b, :], adj_t[:, m, :], start=m == 0, stop=m == TT - 1)
                    last.then_inc(agg2_ps, 1)
                for k in range(2):
                    pe.wait_ge(agg2_tail, 2 * i + k + 1)
                    pe.wait_ge(h_tail, 2 * i + k + 1)
                    for c in range(2):
                        dst = ps[:, 4 + 2 * k + c, :]
                        cols = slice(c * BANK, (c + 1) * BANK)
                        pe.matmul(dst, bg_r[:, 0, :], rs_rows[:, :, :], start=True, stop=False, skip_group_check=True)
                        last = three(dst, wg_hi[:, 0, :], wg_lo[:, 0, :], agg_hi[:, k, cols], agg_lo[:, k, cols], False, True)
                    last.then_inc(r_ps, 1)
                for k in range(2):
                    pe.wait_ge(r_tail, 2 * i + k + 1)
                    for n in range(GB * TT):
                        cols = slice(n * P, (n + 1) * P)
                        dst = ps[:, 2 * k + n // 4, (n % 4) * P:(n % 4 + 1) * P]
                        pe.matmul(dst, r_hi[:, k, cols], wg_hi[:, 1, :], start=True, stop=False, skip_group_check=True)
                        pe.matmul(dst, r_hi[:, k, cols], wg_lo[:, 1, :], start=False, stop=False, skip_group_check=True)
                        last = pe.matmul(dst, r_lo[:, k, cols], wg_hi[:, 1, :], start=False, stop=True, skip_group_check=True)
                    last.then_inc(u_ps, 1)
                for k in range(2):
                    pe.wait_ge(u_tail, 2 + 2 * i + k + 1)
                    for c in range(2):
                        pe.matmul(ps[:, 4 + 2 * k + c, :], bg_r[:, 1, :], rs_rows[:, :, :],
                                  start=True, stop=False, skip_group_check=True)
                    for b in range(GB):
                        for m in range(TT):
                            cols = slice(b * N + m * P, b * N + (m + 1) * P)
                            last = three(ps[:, 4 + 2 * k + b // 2, (b % 2) * N:(b % 2 + 1) * N],
                                         agg_hi[:, k, cols], agg_lo[:, k, cols],
                                         adj_hi[:, m, :], adj_lo[:, m, :], False, m == TT - 1)
                    last.then_inc(h_ps, 1)

            pe.wait_ge(h_tail, 2 + NG)
            with pe.Fori(0, 2) as half:
                for n, (w, s, first, count) in enumerate(STEPS):
                    cols = count * GB
                    with pe.Fori(0, 2) as j:
                        unit, _ = steps_of_pair(half, j, n)
                        for k in range(2):
                            g = half * HALF + 2 * j + k
                            x_hi, x_lo = (seq(t, g, w, s, first, count) for t in (h_hi, h_lo))
                            if n == 0:
                                pe.wait_ge(row_ready, half * HALF + 2)
                            pe.wait_ge(o_ready, unit + k + 1)
                            if s == 0 and w > 1:
                                pe.wait_ge(h_done, 2 + unit + k - HALF + 1)
                            order = (0, 2, 1, 3) if s else (0, 2, 3)
                            for q in order:
                                last = three(ps[:, 4 * k + q, 0:cols], wl_hi[:, w - 1, q, :], wl_lo[:, w - 1, q, :],
                                             x_hi, x_lo, True, s == 0)
                            if s:
                                pe.wait_ge(h_done, 2 + unit + k - HALF + 1)
                                m_hi, m_lo = mid_hi[:, 2 * j + k, 0:cols], mid_lo[:, 2 * j + k, 0:cols]
                                for q in order:
                                    last = three(ps[:, 4 * k + q, 0:cols], wl_hi[:, SKIP + w - 2, q, :],
                                                 wl_lo[:, SKIP + w - 2, q, :], m_hi, m_lo, False, True)
                            last.then_inc(gates_ps, 1)
                with pe.Fori(0, 2) as j:
                    for k in range(2):
                        done = half * HALF + 2 * j + k
                        pe.wait_ge(sum_ready, done + 1)
                        pe.wait_ge(o_ready, (half + 1) * UNITS + 2)
                        pe.wait_ge(row_ready, done + 1)
                        for t in range(TT):
                            for b in range(GB):
                                last = pe.transpose(ps[:, 2 * k + t, b * D:(b + 1) * D],
                                                    h_sum[:, k, b * N + t * P:b * N + (t + 1) * P], ident[:, :])
                        last.then_inc(out_ps, 1)

        @block.scalar
        def _(act):
            act.sem_inc(z1_sb, 2)
            act.sem_inc(o_ready, 2)

            def sqrt(n, width):
                act.wait_ge(var_ready, n + 1)
                act.activation(tmp[:, 1, 0:width], tmp[:, 0, 0:width], ACT.Sqrt).then_inc(sd_ready, 1)

            def normalise(c, k, done):
                for t in range(TT):
                    for b in range(GB):
                        n = t * CB + k * GB + b
                        last = act.activation(normed[:, k, t, b, :], x_row[:, t, c * CB + k * GB + b, :], ACT.Relu,
                                              bias=shift[:, c, n:n + 1], scale=rstd[:, c, n:n + 1])
                last.then_inc(done, 1)

            def both(first):
                return banks(first).rearrange("p a c -> p (a c)")

            sqrt(0, TT)
            sqrt(1, CG)
            act.wait_ge(stat_ready, 1)
            for k in range(2):
                normalise(0, k, normed_ready)
            for c in range(1, CHUNKS):
                sqrt(1 + c, CG)

            def first_half(i, more):
                for k in range(2):
                    act.wait_ge(agg_ps, 2 * i + k + 1)
                    act.activation(agg_hi[:, k, :], both(2 * k), ACT.Copy).then_inc(agg_head, 1)
                if more:
                    act.wait_ge(stat_ready, i + 2)
                for k in range(2):
                    for hh in range(HH):
                        act.wait_ge(z1_ps, 2 * (2 * i + k) + hh + 1)
                        act.activation(z1[:, hh, 2 * i + k, :], both(4 + 2 * hh), ACT.Copy).then_inc(z1_sb, 1)
                    if more:
                        normalise(i + 1, k, normed_ready)

            with act.Fori(0, CHUNKS - 1) as i:
                first_half(i, True)
            first_half(CHUNKS - 1, False)
            sqrt(1 + CHUNKS, HH)
            for n in range(NMAT):
                act.wait_ge(wl_ps, n + 1)
                act.activation(wl_hi[:, n, :, :].rearrange("p q c -> p (q c)"), ps[:, n % 4, :], ACT.Copy).then_inc(wl_head, 1)
            act.wait_ge(bn1_ready, 1)
            with act.Fori(0, CHUNKS) as i:
                for k in range(2):
                    for hh in range(HH):
                        v = z1[:, hh, 2 * i + k, :]
                        last = act.activation(v, v, ACT.Relu, bias=sh_a[:, hh:hh + 1], scale=sc_a[:, hh:hh + 1])
                    last.then_inc(hid_ready, 1)
            sqrt(2 + CHUNKS, 1)
            act.wait_ge(bn2_ready, 1)
            with act.Fori(0, CHUNKS) as i:
                for k in range(2):
                    act.wait_ge(y_ps, 2 * i + k + 1)
                    act.activation(y_col[:, k, :], z2[:, 2 * i + k, :], ACT.Identity,
                                   bias=sh_a[:, 2:3], scale=sc_a[:, 2:3]).then_inc(y_ready, 1)
                sqrt(3 + CHUNKS + i, CG)

            def graph_layers(i, more):
                for k in range(2):
                    act.wait_ge(agg2_ps, 2 * i + k + 1)
                    act.activation(agg_hi[:, k, :], both(2 * k), ACT.Copy).then_inc(agg2_head, 1)
                for k in range(2):
                    act.wait_ge(r_ps, 2 * i + k + 1)
                    act.activation(r_hi[:, k, :], both(4 + 2 * k), ACT.Relu).then_inc(r_head, 1)
                if more:
                    normalise(i + 1, 0, normed2_ready)
                for k in range(2):
                    act.wait_ge(u_ps, 2 * i + k + 1)
                    act.activation(agg_hi[:, k, :], both(2 * k), ACT.Copy).then_inc(u_head, 1)
                if more:
                    normalise(i + 1, 1, normed2_ready)
                for k in range(2):
                    act.wait_ge(h_ps, 2 * i + k + 1)
                    act.activation(h_hi[:, 2 * i + k, :].rearrange("p (t b) -> p t b", b=GB),
                                   both(4 + 2 * k).rearrange("p (b t) -> p t b", b=GB), ACT.Relu).then_inc(h_head, 1)

            act.wait_ge(stat2_ready, CHUNKS)
            for k in range(2):
                normalise(0, k, normed2_ready)
            with act.Fori(0, CHUNKS - 1) as i:
                graph_layers(i, True)
            graph_layers(CHUNKS - 1, False)

            with act.Fori(0, 2) as half:
                for n, (w, s, first, count) in enumerate(STEPS):
                    cols = count * GB

                    def function(k, q, func):
                        col = (w - 1) * GATES + q
                        return act.activation(gate[:, k, q, 0:cols], ps[:, 4 * k + q, 0:cols], func,
                                              bias=lbias[:, col:col + 1])

                    with act.Fori(0, 2) as j:
                        unit, _ = steps_of_pair(half, j, n)
                        for k in range(2):
                            act.wait_ge(gates_ps, unit + k + 1)
                            act.wait_ge(h_done, unit + k + 1)
                            function(k, 0, ACT.Sigmoid)
                            function(k, 2, ACT.Tanh).then_inc(ig_ready, 1)
                            if s:
                                function(k, 1, ACT.Sigmoid).then_inc(f_ready, 1)
                            function(k, 3, ACT.Sigmoid).then_inc(o_ready, 1)
                        for k in range(2):
                            act.wait_ge(c_ready, unit + k + 1)
                            act.activation(gate[:, k, 2, 0:cols], cell[:, 2 * j + k, 0:cols], ACT.Tanh).then_inc(tc_ready, 1)

        @block.vector
        def _(dve):
            for s in (agg_tail, z2_sb, x1_ready, u_tail, h_tail, h_done, row_ready):
                dve.sem_inc(s, 2)
            links = {"value": 0, "count": 0}

            def link(instruction):
                links["value"] = links["value"] + 1
                links["count"] += 1
                instruction.then_inc(step, 1)
                dve.wait_ge(step, links["value"])

            def rsqrt(n, width, dst):
                v, sd, r, e, c = (tmp[:, t, 0:width] for t in range(5))
                dve.wait_ge(sd_ready, n + 1)
                link(dve.reciprocal(r, sd))
                link(dve.tensor_tensor(e, r, r, ALU.mult))
                link(dve.tensor_tensor(e, e, v, ALU.mult))
                link(dve.tensor_scalar(c, e, -0.5, 1.5, ALU.mult, ALU.add))
                link(dve.tensor_tensor(dst, r, c, ALU.mult))

            def split(head, tail, src):
                link(dve.tensor_copy(head, src))
                return dve.tensor_tensor(tail, src, head.bitcast(F32), ALU.subtract)

            LN_LINKS = 11

            def layernorm_stats(c, n, done):
                for t in range(TT):
                    for b in range(CB):
                        last = dve.bn_stats(lnst[:, t * CB + b, :], x_row[:, t, c * CB + b, :])
                link(last)
                even, odd, mean2 = lnst[:, :, 1], lnst[:, :, 4], tmp[:, 5, :]
                link(dve.tensor_tensor(mean2, even, odd, ALU.add))
                link(dve.tensor_tensor(tmp[:, 6, :], even, odd, ALU.subtract))
                link(dve.tensor_tensor(tmp[:, 6, :], tmp[:, 6, :], tmp[:, 6, :], ALU.mult))
                link(dve.tensor_tensor(tmp[:, 7, :], lnst[:, :, 2], lnst[:, :, 5], ALU.add))
                link(dve.tensor_scalar(tmp[:, 7, :], tmp[:, 7, :], 1.0 / D, EPS, ALU.mult, ALU.add))
                dve.scalar_tensor_tensor(out=tmp[:, 0, :], in0=tmp[:, 6, :], scalar=0.25, in1=tmp[:, 7, :],
                                         op0=ALU.mult, op1=ALU.add).then_inc(var_ready, 1)
                rsqrt(n, CG, rstd[:, c, :])
                dve.scalar_tensor_tensor(out=shift[:, c, :], in0=mean2, scalar=-0.5, in1=rstd[:, c, :],
                                         op0=ALU.mult, op1=ALU.mult).then_inc(done, 1)

            def batchnorm_affine(n, stats, first, width, rows, done):
                bias, gamma, beta = (vec[:, r:r + width] for r in rows)
                for k, s in enumerate(stats):
                    last = dve.bn_aggr(mv[:, first + k, :], s)
                link(last)
                mean, var = mv[:, first:first + width, 0], mv[:, first:first + width, 1]
                mu, d = tmp[:, 5, 0:width], tmp[:, 6, 0:width]
                scale, shift_ = sc_a[:, first:first + width], sh_a[:, first:first + width]
                dve.tensor_scalar(tmp[:, 0, 0:width], var, EPS, None, ALU.add).then_inc(var_ready, 1)
                link(dve.tensor_tensor(mu, mean, bias, ALU.add))
                link(dve.tensor_tensor(d, bias, mu, ALU.subtract))
                rsqrt(n, width, scale)
                link(dve.tensor_tensor(scale, scale, gamma, ALU.mult))
                link(dve.tensor_tensor(d, d, scale, ALU.mult))
                dve.tensor_tensor(shift_, d, beta, ALU.add).then_inc(done, 1)

            def both(first):
                return banks(first).rearrange("p a c -> p (a c)")

            row, col, diag, total = (deg[:, k, :] for k in range(4))
            dinv = row
            dve.wait_ge(const_ready, 5)
            dve.wait_ge(ld_adj, 16)
            dve.reduce_sum(row, raw_a[:, :, :], axis=AX.X)
            for t in range(TT):
                block_ = slice(t * P, (t + 1) * P)
                link(dve.tensor_tensor(a_norm[:, t, block_], raw_a[:, t, block_], ident[:, :], ALU.mult))
                link(dve.reduce_sum(diag[:, t:t + 1], a_norm[:, t, block_], axis=AX.X))
            dve.wait_ge(setup_ps, 1)
            dve.tensor_copy(adj_t[:, :, :].rearrange("p t n -> p (t n)"), ps[:, 0, :]).then_inc(setup_sb, 1)
            dve.wait_ge(setup_sb, 1)
            link(dve.reduce_sum(col, adj_t[:, :, :], axis=AX.X))
            link(dve.scalar_tensor_tensor(out=total, in0=row, scalar=1.0, in1=col, op0=ALU.add, op1=ALU.add))
            dve.tensor_tensor(tmp[:, 0, 0:TT], total, diag, ALU.subtract).then_inc(var_ready, 1)
            link(dve.tensor_copy(a_norm[:, :, :], raw_a[:, :, :]))
            for t in range(TT):
                block_ = slice(t * P, (t + 1) * P)
                link(dve.tensor_tensor(a_norm[:, t, block_], a_norm[:, t, block_], ident[:, :], ALU.add))
            rsqrt(0, TT, dinv)
            for t in range(TT):
                last = dve.tensor_scalar(a_norm[:, t, :], a_norm[:, t, :], dinv[:, t:t + 1], None, ALU.mult)
            last.then_inc(setup_sb, 1)
            dve.wait_ge(setup_ps, 2)
            w1_ps = ps[:, 1, 0:HH * P].rearrange("p (k c) -> p k c", k=HH)
            split(w1_hi[:, :, :], w1_lo[:, :, :], w1_ps)
            dve.tensor_copy(w2_t[:, :, :], ps[:, 1, HH * P:2 * HH * P].rearrange("p (k c) -> p k c", k=HH))
            dve.wait_ge(setup_ps, 3)
            link(dve.tensor_copy(vec[:, :], ps[:, 2, 0:ROWS]))
            dve.tensor_tensor(lbias[:, :], vec[:, R_BIH:R_BIH + SKIP * GATES], vec[:, R_BHH:R_BHH + SKIP * GATES], ALU.add)
            split(adj_hi[:, :, :], adj_lo[:, :, :], adj_t[:, :, :])
            split(wg_hi[:, :, :], wg_lo[:, :, :], raw_g[:, :, :])
            dve.wait_ge(ld_bg, 16 * 6)
            link(split(bg_r[:, :, :], bg_l[:, :, :], raw_bg[:, :, :]))
            dve.tensor_copy(bg_r[64:65, :, :], bg_l[64:65, :, :].bitcast(F32))
            dve.wait_ge(setup_ps, 4)
            link(split(rs_r[:, :], rs_l[:, :], ps[:, 3, 0:N]))
            for c in range(2):
                dve.tensor_copy(rs_rows[0:1, c, :], rs_r[0:1, :].bitcast(F32))
                dve.tensor_copy(rs_rows[32:33, c, :], rs_l[32:33, :].bitcast(F32))
                dve.tensor_copy(rs_rows[64:65, c, :], rs_r[64:65, :].bitcast(F32))
            dve.wait_ge(setup_ps, 5)
            for m in range(TT):
                last = dve.tensor_scalar(ahat_t[:, m, :], ps[:, 4, m * N:(m + 1) * N], dinv[:, m:m + 1], None, ALU.mult)
            last.then_inc(setup_sb, 1)

            start = links["value"]
            with dve.Fori(0, CHUNKS) as c:
                links["value"], links["count"] = c * LN_LINKS + start, 0
                dve.wait_ge(x_landed, c + 1)
                layernorm_stats(c, 1 + c, stat_ready)
                assert links["count"] == LN_LINKS
            links["value"] = start + CHUNKS * LN_LINKS

            with dve.Fori(0, CHUNKS) as i:
                for k in range(2):
                    dve.wait_ge(agg_head, 2 * i + k + 1)
                    dve.tensor_tensor(agg_lo[:, k, :], both(2 * k), agg_hi[:, k, :].bitcast(F32),
                                      ALU.subtract).then_inc(agg_tail, 1)
                for k in range(2):
                    for hh in range(HH):
                        dve.wait_ge(z1_sb, 2 + 2 * (2 * i + k) + hh + 1)
                        for c in range(2):
                            dve.bn_stats(st1[:, hh, 2 * (2 * i + k) + c, :],
                                         z1[:, hh, 2 * i + k, c * BANK:(c + 1) * BANK]).then_inc(step, 1)
            links["value"] = links["value"] + NG * HH * 2
            dve.wait_ge(step, links["value"])
            batchnorm_affine(1 + CHUNKS, [st1[:, hh, :, :] for hh in range(HH)], 0, HH, (R_B1, R_G1, R_BE1), bn1_ready)
            for n in range(NMAT):
                dve.wait_ge(wl_head, n + 1)
                dve.tensor_tensor(wl_lo[:, n, :, :].rearrange("p q c -> p (q c)"), ps[:, n % 4, :],
                                  wl_hi[:, n, :, :].rearrange("p q c -> p (q c)").bitcast(F32),
                                  ALU.subtract).then_inc(wl_done, 1)

            with dve.Fori(0, CHUNKS) as i:
                for k in range(2):
                    dve.wait_ge(z2_ps, 2 * i + k + 1)
                    dve.tensor_copy(z2[:, 2 * i + k, :], both(4 + 2 * k)).then_inc(z2_sb, 1)
                    dve.wait_ge(z2_sb, 2 + 2 * i + k + 1)
                    for c in range(2):
                        dve.bn_stats(st2[:, 2 * (2 * i + k) + c, :],
                                     z2[:, 2 * i + k, c * BANK:(c + 1) * BANK]).then_inc(step, 1)
            links["value"] = links["value"] + NG * 2
            dve.wait_ge(step, links["value"])
            batchnorm_affine(2 + CHUNKS, [st2[:, :, :]], HH, 1, (R_B2, R_G2, R_BE2), bn2_ready)

            start = links["value"]
            with dve.Fori(0, CHUNKS) as i:
                links["value"], links["count"] = i * LN_LINKS + start, 0
                for k in range(2):
                    dve.wait_ge(y_ps, 2 + 2 * i + k + 1)
                    g4 = x_row[:, :, bass.ds((2 * i + k) * GB, GB), :]
                    dve.tensor_tensor(g4, banks(4 + 2 * k).rearrange("p t (b d) -> p t b d", b=GB), g4,
                                      ALU.add).then_inc(x1_ready, 1)
                dve.wait_ge(x1_ready, 2 + 2 * i + 2)
                layernorm_stats(i, 3 + CHUNKS + i, stat2_ready)
            links["value"] = start + CHUNKS * LN_LINKS

            with dve.Fori(0, CHUNKS) as i:
                for k in range(2):
                    dve.wait_ge(agg2_head, 2 * i + k + 1)
                    dve.tensor_tensor(agg_lo[:, k, :], both(2 * k), agg_hi[:, k, :].bitcast(F32),
                                      ALU.subtract).then_inc(agg2_tail, 1)
                for k in range(2):
                    dve.wait_ge(r_head, 2 * i + k + 1)
                    dve.scalar_tensor_tensor(out=r_lo[:, k, :], in0=both(4 + 2 * k), scalar=0.0,
                                             in1=r_hi[:, k, :].bitcast(F32), op0=ALU.max,
                                             op1=ALU.subtract).then_inc(r_tail, 1)
                for k in range(2):
                    dve.wait_ge(u_head, 2 * i + k + 1)
                    dve.tensor_tensor(agg_lo[:, k, :], both(2 * k), agg_hi[:, k, :].bitcast(F32),
                                      ALU.subtract).then_inc(u_tail, 1)
                for k in range(2):
                    dve.wait_ge(h_head, 2 * i + k + 1)
                    head = h_hi[:, 2 * i + k, :].rearrange("p (t b) -> p t b", b=GB)
                    dve.scalar_tensor_tensor(out=h_lo[:, 2 * i + k, :].rearrange("p (t b) -> p t b", b=GB),
                                             in0=both(4 + 2 * k).rearrange("p (b t) -> p t b", b=GB), scalar=0.0,
                                             in1=head.bitcast(F32), op0=ALU.max, op1=ALU.subtract).then_inc(h_tail, 1)

            PRODUCTS = sum((3 if s else 2) for _, s, _, _ in STEPS) * HALF
            start = links["value"]
            with dve.Fori(0, 2) as half:
                before = 0
                for n, (w, s, first, count) in enumerate(STEPS):
                    cols = count * GB
                    per_pair = 2 * (3 if s else 2)
                    with dve.Fori(0, 2) as j:
                        links["value"] = start + half * PRODUCTS + (before + j * per_pair)
                        links["count"] = 0
                        unit, carried = steps_of_pair(half, j, n)
                        for k in range(2):
                            i_, f_, g_ = (gate[:, k, q, 0:cols] for q in range(3))
                            c_ = cell[:, 2 * j + k, 0:cols]
                            dve.wait_ge(ig_ready, unit + k + 1)
                            if s == 0:
                                dve.tensor_tensor(c_, i_, g_, ALU.mult).then_inc(c_ready, 1)
                            else:
                                dve.tensor_tensor(i_, i_, g_, ALU.mult)
                                dve.wait_ge(f_ready, carried + k + 1)
                                link(dve.tensor_tensor(f_, f_, c_, ALU.mult))
                                dve.tensor_tensor(c_, i_, f_, ALU.add).then_inc(c_ready, 1)
                        for k in range(2):
                            g = half * HALF + 2 * j + k
                            tc_, o_ = gate[:, k, 2, 0:cols], gate[:, k, 3, 0:cols]
                            dve.wait_ge(tc_ready, unit + k + 1)
                            link(dve.tensor_tensor(o_, o_, tc_, ALU.mult))
                            if s == w - 1:
                                hi, lo = (seq(t, g, w, s, first, count) for t in (h_hi, h_lo))
                                o_ = o_.rearrange("p (t b) -> p t b", b=GB)
                            else:
                                hi, lo = mid_hi[:, 2 * j + k, 0:cols], mid_lo[:, 2 * j + k, 0:cols]
                            split(hi, lo, o_).then_inc(h_done, 1)
                        assert links["count"] == per_pair
                    before += 2 * per_pair
                with dve.Fori(0, 2) as j:
                    for k in range(2):
                        done = half * HALF + 2 * j + k
                        dve.wait_ge(out_ps, 2 + done + 1)
                        dve.wait_ge(out_done[k], 16 * TT * (half * 2 + j + 1))
                        dve.tensor_tensor(o_row[:, k, :, :, :], banks(2 * k).rearrange("p t (b d) -> p t b d", b=GB),
                                          x_row[:, :, bass.ds(done * GB, GB), :], ALU.add).then_inc(row_ready, 1)


_INS = ['x', 'adj', 'L0_gnn_W1', 'L0_gnn_b1', 'L0_gnn_g1', 'L0_gnn_be1', 'L0_gnn_W2', 'L0_gnn_b2', 'L0_gnn_g2',
        'L0_gnn_be2', 'L1_gnn_Wg0', 'L1_gnn_bg0', 'L1_gnn_Wg1', 'L1_gnn_bg1', 'L1_gnn_Wih', 'L1_gnn_Whh',
        'L1_gnn_bih', 'L1_gnn_bhh']


def kernel(**inputs):
    import numpy as _np
    import concourse.bacc as _bacc
    from concourse import mybir as _mybir
    from concourse.bass_utils import run_bass_kernel_spmd as _run

    nc = _bacc.Bacc("TRN2", target_bir_lowering=False, num_devices=1)
    arrays, args = {}, []
    for name in _INS:
        a = _np.ascontiguousarray(inputs[name])
        arrays[f"in_{name}_dram"] = a
        args.append(nc.dram_tensor(f"in_{name}_dram", a.shape, _mybir.dt.from_np(a.dtype), kind="ExternalInput").ap())
    shape = arrays["in_x_dram"].shape
    args.append(nc.dram_tensor("out_0_dram", shape, _mybir.dt.from_np(_np.dtype("float32")), kind="ExternalOutput").ap())
    gnn_lstm_kernel(nc, *args)
    r = _run(nc, [arrays], core_ids=[0])
    return r.results[0]["out_0_dram"]
```

```python
import concourse.bass as bass
from concourse import mybir
from contextlib import ExitStack

F32 = mybir.dt.float32
F32R = mybir.dt.float32r
ALU = mybir.AluOpType
ACT = mybir.ActivationFunctionType
AX = mybir.AxisListType

P = 128
KIB = 1024


def gnn_lstm_kernel(nc, x, adj, W1, b1, g1, be1, W2, b2, g2, be2,
                    Wg0, bg0, Wg1, bg1, Wih, Whh, bih, bhh, out):
    B, N, D = x.shape
    TT = N // P
    HH = W1.shape[0] // P
    GB = 4
    NG = B // GB
    GC = GB * N
    BANK = 512
    CHUNKS = NG // 2
    CB = 2 * GB
    SKIP = Wih.shape[0]
    GATES = Wih.shape[1] // P
    RG = TT * GB
    EPS = 1e-5
    R_B1, R_G1, R_BE1 = 0, HH, 2 * HH
    R_B2, R_G2, R_BE2 = 3 * HH, 3 * HH + 1, 3 * HH + 2
    R_BIH = 3 * HH + 3
    R_BHH = R_BIH + SKIP * GATES
    ROWS = R_BHH + SKIP * GATES

    ctx = ExitStack()
    with ctx:
        base = -(-nc.sbuf_base // 64) * 64

        def row_bytes(shape):
            n = 4
            for d in shape[1:]:
                n *= d
            return n

        def at(name, shape, dt, offset):
            return nc.alloc_sbuf_tensor_at(name, shape, dt, offset=base + offset)

        NMAT = 2 * SKIP - 1
        HALF = NG // 2
        AT_X, AT_Z, AT_Z2, AT_WL, AT_Y, AT_S, AT_R, AT_SMALL = (
            k * KIB for k in (0, 32, 96, 128, 156, 164, 180, 196))
        x_row = at("x_row", [P, TT, B, D], F32, AT_X)
        z1 = at("z1", [P, HH, NG, GC], F32, AT_Z)
        h_hi = at("h_hi", [P, NG, GC], F32R, AT_Z)
        h_lo = at("h_lo", [P, NG, GC], F32R, AT_Z + 32 * KIB)
        z2 = at("z2", [P, NG, GC], F32, AT_Z2)
        agg_hi = at("agg_hi", [P, 2, GC], F32R, AT_Z2)
        agg_lo = at("agg_lo", [P, 2, GC], F32R, AT_Z2 + 8 * KIB)
        ones = at("ones", [P, P], F32, AT_Z2 + 16 * KIB)
        rs_r = at("rs_r", [P, N], F32R, AT_Z2 + 17 * KIB)
        rs_l = at("rs_l", [P, N], F32R, AT_Z2 + 18 * KIB)
        bg_l = at("bg_l", [P, 2, P], F32R, AT_Z2 + 19 * KIB)
        ahat_t = at("ahat_t", [P, TT, N], F32, AT_Z2 + 20 * KIB)
        w1_hi = at("w1_hi", [P, HH, P], F32R, AT_Z2 + 22 * KIB)
        w1_lo = at("w1_lo", [P, HH, P], F32R, AT_Z2 + 23 * KIB)
        adj_t = at("adj_t", [P, TT, N], F32, AT_Z2 + 24 * KIB)
        mid_hi = at("mid_hi", [P, HALF, BANK], F32R, AT_Z2)
        mid_lo = at("mid_lo", [P, HALF, BANK], F32R, AT_Z2 + 8 * KIB)
        cell = at("cell", [P, HALF, BANK], F32, AT_Z2 + 16 * KIB)
        o_row = at("o_row", [P, 2, TT, GB, D], F32, AT_Z2 + 24 * KIB)
        wl_hi = at("wl_hi", [P, NMAT, GATES, P], F32R, AT_WL)
        wl_lo = at("wl_lo", [P, NMAT, GATES, P], F32R, AT_WL + NMAT * 2 * KIB)
        normed = at("normed", [P, 2, TT, GB, D], F32, AT_Y)
        y_col = at("y_col", [P, 2, GC], F32, AT_Y)
        s_hi = at("s_hi", [P, 2, GC], F32R, AT_S)
        s_lo = at("s_lo", [P, 2, GC], F32R, AT_S + 8 * KIB)
        r_hi = at("r_hi", [P, 2, GC], F32R, AT_R)
        r_lo = at("r_lo", [P, 2, GC], F32R, AT_R + 8 * KIB)
        gate = at("gate", [P, HALF, GATES, BANK], F32, AT_Y)
        st1 = at("st1", [P, HH, 2 * NG, 6], F32, AT_S)
        st2 = at("st2", [P, 2 * NG, 6], F32, AT_S + KIB)
        w2_t = at("w2_t", [P, HH, P], F32, AT_S + 2 * KIB)
        raw_a = at("raw_a", [P, TT, N], F32, AT_S + 3 * KIB)
        a_norm = at("a_norm", [P, TT, N], F32, AT_S + 5 * KIB)
        raw_1 = at("raw_1", [P, HH, D], F32, AT_S + 7 * KIB)
        raw_2 = at("raw_2", [P, HH * P], F32, AT_S + 8 * KIB)
        raw_g = at("raw_g", [P, 2, D], F32, AT_S + 9 * KIB)
        raw_bg = at("raw_bg", [P, 2, D], F32, AT_S + 10 * KIB)
        raw_v = at("raw_v", [ROWS, D], F32, AT_S + 11 * KIB)
        raw_l = at("raw_l", [P, NMAT, GATES, D], F32, AT_R)
        small = {"at": AT_SMALL}

        def sb(name, shape, dt=F32):
            t = at(name, shape, dt, small["at"])
            small["at"] += -(-row_bytes(shape) // 32) * 32
            return t

        ident = sb("ident", [P, P])
        ident_r = sb("ident_r", [P, P], F32R)
        adj_hi = sb("adj_hi", [P, TT, N], F32R)
        adj_lo = sb("adj_lo", [P, TT, N], F32R)
        wg_hi = sb("wg_hi", [P, 2, P], F32R)
        wg_lo = sb("wg_lo", [P, 2, P], F32R)
        bg_r = sb("bg_r", [P, 2, P], F32R)
        rs_rows = sb("rs_rows", [P, N], F32R)
        vec = sb("vec", [P, ROWS])
        lbias = sb("lbias", [P, SKIP * GATES])
        mv = sb("mv", [P, 3, 2])
        sc_a = sb("sc_a", [P, 3])
        sh_a = sb("sh_a", [P, 3])
        deg = sb("deg", [P, 5, TT])
        bnt = sb("bnt", [P, 4, HH])
        powers = sb("powers", [P, RG])
        lnst = sb("lnst", [P, 2, RG, 6])
        lnt = sb("lnt", [P, 2, 6, RG])
        rstd = sb("rstd", [P, 2, RG])
        shift = sb("shift", [P, 2, RG])
        ps = ctx.enter_context(nc.psum_tensor("ps", [P, 8, BANK], F32))

        def both(first):
            return ps[:, first:first + 2, :].rearrange("p a c -> p (a c)")

        def sem(name):
            return ctx.enter_context(nc.semaphore(name))

        ld_adj, ld_w1, ld_w, ld_vec, ld_bg, ld_lstm = (sem(n) for n in ("ld_adj", "ld_w1", "ld_w", "ld_vec", "ld_bg", "ld_lstm"))
        ld_x = [sem(f"ld_x{c}") for c in range(CHUNKS)]
        x_landed = sem("x_landed")
        const_ready = sem("const_ready")
        setup_ps = sem("setup_ps")
        setup_sb = sem("setup_sb")
        rs_ps = sem("rs_ps")
        rs_read = sem("rs_read")
        ident_ready = sem("ident_ready")
        wl_ps, wl_head, wl_done = sem("wl_ps"), sem("wl_head"), sem("wl_done")
        step = sem("step")
        pstep = sem("pstep")
        var_ready, root_ready = sem("var_ready"), sem("root_ready")
        st_ready, stat_ready = sem("st_ready"), sem("stat_ready")
        normed_ready, agg_ps, agg_head, agg_tail = (sem(n) for n in ("normed_ready", "agg_ps", "agg_head", "agg_tail"))
        z1_ps, z1_sb = sem("z1_ps"), sem("z1_sb")
        bn1_ready, bn2_ready = sem("bn1_ready"), sem("bn2_ready")
        hid_ready, z2_ps, z2_sb = sem("hid_ready"), sem("z2_ps"), sem("z2_sb")
        y_ready, y_ps, x1_ready = sem("y_ready"), sem("y_ps"), sem("x1_ready")
        n_ready, n_head, n_tail = sem("n_ready"), sem("n_head"), sem("n_tail")
        agg2_ps, agg2_head, agg2_tail = (sem(n) for n in ("agg2_ps", "agg2_head", "agg2_tail"))
        r_ps, r_head, r_tail = sem("r_ps"), sem("r_head"), sem("r_tail")
        u_ps, u_head, u_tail = sem("u_ps"), sem("u_head"), sem("u_tail")
        h_ps, h_head, h_tail = sem("h_ps"), sem("h_head"), sem("h_tail")
        gates_ps = sem("gates_ps")
        ig_ready, f_ready, o_ready = sem("ig_ready"), sem("f_ready"), sem("o_ready")
        c_ready, tc_ready, h_done = sem("c_ready"), sem("tc_ready"), sem("h_done")
        out_ps, row_ready = sem("out_ps"), sem("row_ready")
        out_done = [sem(f"out_done{k}") for k in range(2)]

        STEPS = []
        for w in range(1, SKIP + 1):
            count = N // w
            parts = -(-count * GB // BANK)
            for s in range(w):
                for c in range(parts):
                    STEPS.append((w, s, c * (count // parts), count // parts))
        UNITS = len(STEPS) * HALF
        CARRIED = sum(s > 0 for _, s, _, _ in STEPS) * HALF

        def seq(t, g, w, s, first, count):
            v = t[:, g, :].rearrange("p (t b) -> p t b", b=GB)
            lo = first * w + s
            return v[:, lo:lo + (count - 1) * w + 1:w, :]

        block = ctx.enter_context(nc.Block())

        @block.sync
        def _(sp):
            def load_x(c):
                for t in range(TT):
                    sp.dma_start(x_row[:, t, c * CB:(c + 1) * CB, :],
                                 x[c * CB:(c + 1) * CB, t * P:(t + 1) * P, :].rearrange("b p d -> p b d")
                                 ).then_inc(ld_x[c], 16)

            sp.dma_start(raw_a[:, :, :], adj.rearrange("(t p) m -> p t m", p=P)).then_inc(ld_adj, 16)
            load_x(0)
            sp.dma_start(raw_1[:, :, :], W1.rearrange("(k p) d -> p k d", p=P)).then_inc(ld_w1, 16)
            load_x(1)
            for row, v in ((R_B1, b1), (R_G1, g1), (R_BE1, be1)):
                sp.dma_start(raw_v[row:row + HH, :], v.rearrange("(k p) -> k p", p=P)).then_inc(ld_vec, 16)
            for row, v in ((R_B2, b2), (R_G2, g2), (R_BE2, be2)):
                sp.dma_start(raw_v[row:row + 1, :], v.rearrange("(k p) -> k p", p=P)).then_inc(ld_vec, 16)
            for row, v in ((R_BIH, bih), (R_BHH, bhh)):
                sp.dma_start(raw_v[row:row + SKIP * GATES, :], v.rearrange("w (q p) -> (w q) p", p=P)).then_inc(ld_vec, 16)
            sp.dma_start(raw_2[:, :], W2).then_inc(ld_w, 16)
            sp.dma_start(raw_g[:, 0, :], Wg0).then_inc(ld_w, 16)
            sp.dma_start(raw_g[:, 1, :], Wg1).then_inc(ld_w, 16)
            for c in range(2, CHUNKS):
                load_x(c)
            for w in range(SKIP):
                sp.dma_start(raw_l[:, w, :, :], Wih[w].rearrange("(q p) d -> p q d", p=P)).then_inc(ld_lstm, 16)
            for w in range(1, SKIP):
                sp.dma_start(raw_l[:, SKIP + w - 1, :, :], Whh[w].rearrange("(q p) d -> p q d", p=P)).then_inc(ld_lstm, 16)
            sp.wait_ge(const_ready, 5)
            for q in (0, 32, 64):
                for layer, v in ((0, bg0), (1, bg1)):
                    sp.dma_start(raw_bg[q:q + 1, layer, :], v.rearrange("(k p) -> k p", p=P)).then_inc(ld_bg, 16)
            for c in range(CHUNKS):
                sp.wait_ge(ld_x[c], 16 * TT)
                sp.sem_inc(x_landed, 1)
            for k in range(2):
                sp.sem_inc(out_done[k], 16 * TT)
            with sp.Fori(0, CHUNKS) as i:
                for k in range(2):
                    sp.wait_ge(row_ready, 2 * i + k + 1)
                    for t in range(TT):
                        sp.dma_start(out[bass.ds(i * CB + k * GB, GB), t * P:(t + 1) * P, :].rearrange("b p d -> p b d"),
                                     o_row[:, k, t, :, :]).then_inc(out_done[k], 16)
            for k in range(2):
                sp.wait_ge(out_done[k], 16 * TT * (CHUNKS + 1))

        @block.gpsimd
        def _(pool):
            pool.memset(ident[:, :], 0.0).then_inc(const_ready, 1)
            pool.wait_ge(const_ready, 1)
            pool.affine_select(out=ident[:, :], in_=ident[:, :], compare_op=ALU.not_equal, fill=1.0,
                               base=0, pattern=[[-1, P]], channel_multiplier=1).then_inc(const_ready, 1)
            pool.memset(raw_bg[:, :, :], 0.0).then_inc(const_ready, 1)
            pool.memset(ones[:, :], 1.0).then_inc(const_ready, 1)
            pool.memset(rs_rows[:, :].bitcast(F32), 0.0).then_inc(const_ready, 1)
            pool.memset(powers[:, :], -0.5).then_inc(const_ready, 1)
            pool.wait_ge(const_ready, 6)

            links = {"value": 0, "count": 0}

            def link(instruction):
                links["value"] = links["value"] + 1
                links["count"] += 1
                instruction.then_inc(pstep, 1)
                pool.wait_ge(pstep, links["value"])

            def root(n, dst, v):
                pool.wait_ge(var_ready, n + 1)
                pool.tensor_tensor(dst, v, powers[:, 0:v.shape[-1]], ALU.pow).then_inc(root_ready, 1)

            LN_LINKS = 4

            def layernorm_stats(n, k):
                even, odd = lnst[:, k, :, 1], lnst[:, k, :, 4]
                mean2, diff, both_, sq, v4, less_mean2 = (lnt[:, k, t, :] for t in range(6))
                half_r = both_
                pool.wait_ge(st_ready, n + 1)
                pool.tensor_tensor(mean2, even, odd, ALU.add)
                pool.tensor_tensor(diff, even, odd, ALU.subtract)
                link(pool.tensor_tensor(both_, lnst[:, k, :, 2], lnst[:, k, :, 5], ALU.add))
                pool.tensor_tensor(sq, diff, diff, ALU.mult)
                pool.tensor_scalar(less_mean2, mean2, -1.0, None, ALU.mult)
                link(pool.tensor_scalar(v4, both_, 4.0 / D, 4.0 * EPS, ALU.mult, ALU.add))
                link(pool.tensor_tensor(v4, v4, sq, ALU.add))
                link(pool.tensor_tensor(half_r, v4, powers[:, :], ALU.pow))
                pool.tensor_tensor(shift[:, k, :], less_mean2, half_r, ALU.mult)
                pool.tensor_scalar(rstd[:, k, :], half_r, 2.0, None, ALU.mult).then_inc(stat_ready, 1)

            def layernorm_groups(first):
                start = links["value"]
                with pool.Fori(0, CHUNKS) as i:
                    for k in range(2):
                        links["value"], links["count"] = i * (2 * LN_LINKS) + (start + k * LN_LINKS), 0
                        layernorm_stats(2 * i + (first + k), k)
                        assert links["count"] == LN_LINKS
                links["value"] = start + NG * LN_LINKS

            root(0, deg[:, 4, :], deg[:, 3, :])
            layernorm_groups(0)
            root(1, bnt[:, 1, 0:HH], bnt[:, 0, 0:HH])
            root(2, bnt[:, 1, 0:1], bnt[:, 0, 0:1])
            layernorm_groups(NG)

        @block.tensor
        def _(pe):
            def three(dst, w_hi, w_lo, m_hi, m_lo, start, stop):
                pe.matmul(dst, w_hi, m_hi, start=start, stop=False, skip_group_check=True)
                pe.matmul(dst, w_hi, m_lo, start=False, stop=False, skip_group_check=True)
                return pe.matmul(dst, w_lo, m_hi, start=False, stop=stop, skip_group_check=True)

            pe.wait_ge(const_ready, 5)
            pe.wait_ge(ld_adj, 16)
            for m in range(TT):
                for n in range(TT):
                    last = pe.transpose(ps[:, 0, m * N + n * P:m * N + (n + 1) * P],
                                        raw_a[:, n, m * P:(m + 1) * P], ident[:, :])
            last.then_inc(setup_ps, 1)
            pe.wait_ge(ld_w1, 16)
            for k in range(HH):
                last = pe.transpose(ps[:, 1, k * P:(k + 1) * P], raw_1[:, k, :], ident[:, :])
            last.then_inc(setup_ps, 1)
            pe.wait_ge(setup_sb, 2)
            for m in range(TT):
                for n in range(TT):
                    last = pe.transpose(ps[:, 4, m * N + n * P:m * N + (n + 1) * P],
                                        a_norm[:, n, m * P:(m + 1) * P], ident[:, :])
            last.then_inc(setup_ps, 1)
            pe.wait_ge(setup_sb, 3)

            with pe.Fori(0, CHUNKS) as i:
                for k in range(2):
                    pe.wait_ge(normed_ready, 2 * i + k + 1)
                    pe.wait_ge(agg_tail, 2 * i + k + 1)
                    for b in range(GB):
                        for m in range(TT):
                            last = pe.matmul(ps[:, 2 * k + b // 2, (b % 2) * N:(b % 2 + 1) * N],
                                             normed[:, k, m, b, :], ahat_t[:, m, :], start=m == 0, stop=m == TT - 1)
                    last.then_inc(agg_ps, 1)
                for k in range(2):
                    pe.wait_ge(agg_tail, 2 + 2 * i + k + 1)
                    for hh in range(HH):
                        pe.wait_ge(z1_sb, 2 * (2 * i + k) + hh + 1)
                        for c in range(2):
                            cols = slice(c * BANK, (c + 1) * BANK)
                            last = three(ps[:, 4 + 2 * hh + c, :], w1_hi[:, hh, :], w1_lo[:, hh, :],
                                         agg_hi[:, k, cols], agg_lo[:, k, cols], True, True)
                        last.then_inc(z1_ps, 1)

            pe.wait_ge(ld_vec, 16 * 8)
            pe.wait_ge(z1_sb, 2 + 2 * NG)
            pe.transpose(ps[:, 5, 0:ROWS], raw_v[:, :], ident[0:ROWS, 0:ROWS]).then_inc(setup_ps, 1)
            pe.wait_ge(ld_w, 48)
            for k in range(HH):
                last = pe.transpose(ps[:, 6, k * P:(k + 1) * P], raw_2[:, k * P:(k + 1) * P], ident[:, :])
            last.then_inc(setup_ps, 1)
            for m in range(TT):
                last = pe.matmul(ps[:, 7, 0:N], ones[:, :], adj_t[:, m, :], start=m == 0, stop=m == TT - 1)
            last.then_inc(rs_ps, 1)

            def transpose_lstm(first, count):
                for n in range(first, first + count):
                    for q in range(GATES):
                        last = pe.transpose(ps[:, n % 4, q * P:(q + 1) * P], raw_l[:, n, q, :], ident[:, :])
                    last.then_inc(wl_ps, 1)

            pe.wait_ge(ld_lstm, 16 * NMAT)
            transpose_lstm(0, 4)

            pe.wait_ge(setup_sb, 4)
            pe.wait_ge(rs_read, 1)
            with pe.Fori(0, CHUNKS) as i:
                for k in range(2):
                    pe.wait_ge(hid_ready, 2 * i + k + 1)
                    pe.wait_ge(z2_sb, 2 * i + k + 1)
                    for c in range(2):
                        for hh in range(HH):
                            last = pe.matmul(ps[:, 4 + 2 * k + c, :], w2_t[:, hh, :],
                                             z1[:, hh, 2 * i + k, c * BANK:(c + 1) * BANK],
                                             start=hh == 0, stop=hh == HH - 1)
                    last.then_inc(z2_ps, 1)
            pe.wait_ge(wl_done, 4)
            transpose_lstm(4, NMAT - 4)

            def rows_again(k):
                for t in range(TT):
                    for b in range(GB):
                        last = pe.transpose(ps[:, 4 + 2 * k + t, b * D:(b + 1) * D],
                                            y_col[:, k, b * N + t * P:b * N + (t + 1) * P], ident[:, :])
                last.then_inc(y_ps, 1)

            for k in range(2):
                pe.wait_ge(y_ready, k + 1)
                rows_again(k)

            def graph_layers(i, more):
                for k in range(2):
                    pe.wait_ge(n_tail, 2 * i + k + 1)
                    for b in range(GB):
                        for m in range(TT):
                            last = three(ps[:, 2 * k + b // 2, (b % 2) * N:(b % 2 + 1) * N],
                                         s_hi[:, k, (m * GB + b) * D:(m * GB + b + 1) * D],
                                         s_lo[:, k, (m * GB + b) * D:(m * GB + b + 1) * D],
                                         adj_hi[:, m, :], adj_lo[:, m, :], m == 0 and b % 2 == 0, m == TT - 1)
                    last.then_inc(agg2_ps, 1)
                if more:
                    for k in range(2):
                        pe.wait_ge(y_ready, 2 * i + 2 + k + 1)
                        pe.wait_ge(h_tail, 2 * i + k + 1)
                        rows_again(k)
                for k in range(2):
                    pe.wait_ge(agg2_tail, 2 * i + k + 1)
                    for c in range(2):
                        dst = ps[:, 2 * k + c, :]
                        for n in range(2):
                            pe.matmul(dst[:, n * N:(n + 1) * N], bg_r[:, 0, :], rs_rows[:, :], start=n == 0, stop=False,
                                      skip_group_check=True)
                        cols = slice(c * BANK, (c + 1) * BANK)
                        last = three(dst, wg_hi[:, 0, :], wg_lo[:, 0, :], s_hi[:, k, cols], s_lo[:, k, cols], False, True)
                    last.then_inc(r_ps, 1)
                for k in range(2):
                    pe.wait_ge(r_tail, 2 * i + k + 1)
                    if more:
                        pe.wait_ge(x1_ready, 2 * i + 2 + k + 1)
                    else:
                        pe.wait_ge(h_tail, 2 * i + k + 1)
                    for n in range(GB * TT):
                        cols = slice(n * P, (n + 1) * P)
                        dst = ps[:, 4 + 2 * k + n // 4, (n % 4) * P:(n % 4 + 1) * P]
                        pe.matmul(dst, r_hi[:, k, cols], wg_hi[:, 1, :], start=True, stop=False, skip_group_check=True)
                        pe.matmul(dst, r_hi[:, k, cols], wg_lo[:, 1, :], start=False, stop=False, skip_group_check=True)
                        last = pe.matmul(dst, r_lo[:, k, cols], wg_hi[:, 1, :], start=False, stop=True, skip_group_check=True)
                    last.then_inc(u_ps, 1)
                for k in range(2):
                    pe.wait_ge(u_tail, 2 * i + k + 1)
                    for c in range(2):
                        for n in range(2):
                            pe.matmul(ps[:, 4 + 2 * k + c, n * N:(n + 1) * N], bg_r[:, 1, :], rs_rows[:, :],
                                      start=n == 0, stop=False, skip_group_check=True)
                    for b in range(GB):
                        for m in range(TT):
                            cols = slice(b * N + m * P, b * N + (m + 1) * P)
                            last = three(ps[:, 4 + 2 * k + b // 2, (b % 2) * N:(b % 2 + 1) * N],
                                         s_hi[:, k, cols], s_lo[:, k, cols],
                                         adj_hi[:, m, :], adj_lo[:, m, :], False, m == TT - 1)
                    last.then_inc(h_ps, 1)

            with pe.Fori(0, CHUNKS - 1) as i:
                graph_layers(i, True)
            graph_layers(CHUNKS - 1, False)

            def unit(half, n, j, k):
                w, s, first, count = STEPS[n]
                cols = count * GB
                u = 2 * j + (half * UNITS + n * HALF + k)
                g = 2 * j + (half * HALF + k)
                x_hi, x_lo = (seq(t, g, w, s, first, count) for t in (h_hi, h_lo))
                order = (0, 2, 1, 3) if s else (0, 2, 3)
                pe.wait_ge(o_ready, u + 1)
                if s == 0 and w > 1:
                    pe.wait_ge(h_done, u + 1)
                for q in order:
                    last = three(ps[:, 4 * k + q, 0:cols], wl_hi[:, w - 1, q, :], wl_lo[:, w - 1, q, :],
                                 x_hi, x_lo, True, s == 0)
                if s:
                    pe.wait_ge(h_done, u + 1)
                    m_hi, m_lo = mid_hi[:, 2 * j + k, 0:cols], mid_lo[:, 2 * j + k, 0:cols]
                    for q in order:
                        last = three(ps[:, 4 * k + q, 0:cols], wl_hi[:, SKIP + w - 2, q, :],
                                     wl_lo[:, SKIP + w - 2, q, :], m_hi, m_lo, False, True)
                last.then_inc(gates_ps, 1)

            def rows_out(g, banks_):
                h_views = [t[:, g, :].rearrange("p (t b) -> p b t", b=GB) for t in (h_hi, h_lo)]
                for t in range(TT):
                    for b in range(GB):
                        for part, v in enumerate(h_views):
                            last = pe.matmul(ps[:, banks_[t], b * D:(b + 1) * D], v[:, b, t * P:(t + 1) * P],
                                             ident_r[:, :], start=part == 0, stop=part == 1, skip_group_check=True)
                last.then_inc(out_ps, 1)

            for half in range(2):
                for n in range(len(STEPS)):
                    if n == 0:
                        for q in range(HALF):
                            if half == 0:
                                pe.wait_ge(h_tail, 2 + (NG if q else 1))
                            else:
                                pe.wait_ge(row_ready, 2)
                                pe.wait_ge(o_ready, 2 + UNITS)
                            unit(half, 0, q // 2, q % 2)
                            if half and q < 2:
                                pe.wait_ge(h_done, 4 + UNITS - 2 + q + 1)
                                pe.wait_ge(row_ready, 2 + q)
                                rows_out(2 + q, (1, 5))
                        continue
                    if half == 1 and n == 3:
                        pe.wait_ge(row_ready, HALF)
                    with pe.Fori(0, 2) as j:
                        for k in range(2):
                            unit(half, n, j, k)
                done = (half + 1) * UNITS
                pe.wait_ge(o_ready, 2 + done - 1)
                for q in range(2):
                    pe.wait_ge(h_done, 4 + done - HALF + q + 1)
                    rows_out(half * HALF + q, (2 * q, 2 * q + 1))
            pe.wait_ge(o_ready, 2 + done)
            for q in range(2, HALF):
                pe.wait_ge(h_done, 4 + done - HALF + q + 1)
                pe.wait_ge(row_ready, HALF + q)
                rows_out(HALF + q, (1, 5))

        @block.scalar
        def _(act):
            act.sem_inc(z1_sb, 2)
            act.sem_inc(o_ready, 2)

            def normalise(i, k, n, *done):
                act.wait_ge(stat_ready, n)
                for t in range(TT):
                    for b in range(GB):
                        m = t * GB + b
                        last = act.activation(normed[:, k, t, b, :], x_row[:, t, i * CB + (k * GB + b), :], ACT.Relu,
                                              bias=shift[:, k, m:m + 1], scale=rstd[:, k, m:m + 1])
                for s in done:
                    last.then_inc(s, 1)

            for k in range(2):
                normalise(0, k, k + 1, normed_ready)

            def first_half(i, more):
                for k in range(2):
                    act.wait_ge(agg_ps, 2 * i + k + 1)
                    act.activation(agg_hi[:, k, :], both(2 * k), ACT.Copy).then_inc(agg_head, 1)
                for k in range(2):
                    for hh in range(HH):
                        act.wait_ge(z1_ps, 2 * (2 * i + k) + hh + 1)
                        act.activation(z1[:, hh, 2 * i + k, :], both(4 + 2 * hh), ACT.Copy).then_inc(z1_sb, 1)
                    if more:
                        normalise(i + 1, k, 2 * i + 2 + k + 1, normed_ready)

            with act.Fori(0, CHUNKS - 1) as i:
                first_half(i, True)
            first_half(CHUNKS - 1, False)

            def lstm_head(n, bank):
                act.wait_ge(wl_ps, n + 1)
                act.activation(wl_hi[:, n, :, :].rearrange("p q c -> p (q c)"), bank, ACT.Copy).then_inc(wl_head, 1)

            act.wait_ge(bn1_ready, 1)
            with act.Fori(0, CHUNKS) as i:
                for k in range(2):
                    for hh in range(HH):
                        v = z1[:, hh, 2 * i + k, :]
                        last = act.activation(v, v, ACT.Relu, bias=sh_a[:, hh:hh + 1], scale=sc_a[:, hh:hh + 1])
                    last.then_inc(hid_ready, 1)
                lstm_head(i, ps[:, i, :])
            for n in range(4, NMAT):
                lstm_head(n, ps[:, n % 4, :])
            act.wait_ge(bn2_ready, 1)

            def batchnormed(i, k):
                act.activation(y_col[:, k, :], z2[:, 2 * i + k, :], ACT.Identity,
                               bias=sh_a[:, 2:3], scale=sc_a[:, 2:3]).then_inc(y_ready, 1)

            def rows_head(i, k):
                act.wait_ge(n_ready, 2 * i + k + 1)
                act.activation(s_hi[:, k, :], normed[:, k, :, :, :].rearrange("p t b d -> p (t b d)"),
                               ACT.Copy).then_inc(n_head, 1)

            def graph_layers(i, more):
                if more:
                    for k in range(2):
                        act.wait_ge(n_tail, 2 * i + k + 1)
                        batchnormed(i + 1, k)
                for k in range(2):
                    act.wait_ge(agg2_ps, 2 * i + k + 1)
                    act.activation(s_hi[:, k, :], both(2 * k), ACT.Copy).then_inc(agg2_head, 1)
                for k in range(2):
                    act.wait_ge(r_ps, 2 * i + k + 1)
                    act.activation(r_hi[:, k, :], both(2 * k), ACT.Relu).then_inc(r_head, 1)
                for k in range(2):
                    act.wait_ge(u_ps, 2 * i + k + 1)
                    act.activation(s_hi[:, k, :], both(4 + 2 * k), ACT.Copy).then_inc(u_head, 1)
                if more:
                    normalise(i + 1, 0, NG + 2 * i + 2 + 1, n_ready)
                for k in range(2):
                    act.wait_ge(h_ps, 2 * i + k + 1)
                    if more:
                        rows_head(i + 1, k)
                    act.activation(h_hi[:, 2 * i + k, :].rearrange("p (t b) -> p t b", b=GB),
                                   both(4 + 2 * k).rearrange("p (b t) -> p t b", b=GB), ACT.Relu).then_inc(h_head, 1)
                    if more and k == 0:
                        normalise(i + 1, 1, NG + 2 * i + 2 + 2, n_ready)

            for k in range(2):
                batchnormed(0, k)
            for k in range(2):
                normalise(0, k, NG + k + 1, n_ready)
                rows_head(0, k)
            with act.Fori(0, CHUNKS - 1) as i:
                graph_layers(i, True)
            graph_layers(CHUNKS - 1, False)

            def tanh_c(u, q, cols):
                act.wait_ge(c_ready, u + 1)
                act.activation(gate[:, q, 2, 0:cols], cell[:, q, 0:cols], ACT.Tanh).then_inc(tc_ready, 1)

            with act.Fori(0, 2) as half:
                before = None
                carried = 0
                for n, (w, s, first, count) in enumerate(STEPS):
                    cols = count * GB
                    for q in range(HALF):
                        k = q % 2
                        u = half * UNITS + (n * HALF + q)

                        def function(f, func):
                            col = (w - 1) * GATES + f
                            return act.activation(gate[:, q, f, 0:cols], ps[:, 4 * k + f, 0:cols], func,
                                                  bias=lbias[:, col:col + 1])

                        act.wait_ge(gates_ps, u + 1)
                        act.wait_ge(h_done, u + 1)
                        function(0, ACT.Sigmoid)
                        function(2, ACT.Tanh).then_inc(ig_ready, 1)
                        if s:
                            function(1, ACT.Sigmoid).then_inc(f_ready, 1)
                        function(3, ACT.Sigmoid).then_inc(o_ready, 1)
                        if before:
                            tanh_c(*before)
                        before = (u, q, cols)
                tanh_c(*before)

        @block.vector
        def _(dve):
            for s in (agg_tail, z2_sb, h_tail):
                dve.sem_inc(s, 2)
            dve.sem_inc(h_done, HALF)
            links = {"value": 0}

            def link(instruction):
                links["value"] = links["value"] + 1
                instruction.then_inc(step, 1)
                dve.wait_ge(step, links["value"])

            def split(head, tail, src):
                link(dve.tensor_copy(head, src))
                return dve.tensor_tensor(tail, src, head.bitcast(F32), ALU.subtract)

            def row_stats(i, k):
                for t in range(TT):
                    for b in range(GB):
                        last = dve.bn_stats(lnst[:, k, t * GB + b, :], x_row[:, t, i * CB + (k * GB + b), :])
                last.then_inc(st_ready, 1)

            def batchnorm_affine(n, stats, first, width, rows, done):
                for k, s in enumerate(stats):
                    last = dve.bn_aggr(mv[:, first + k, :], s)
                link(last)
                mean, var = mv[:, first:first + width, 0], mv[:, first:first + width, 1]
                v, root, mu, d = (bnt[:, t, 0:width] for t in range(4))
                scale, shift_ = sc_a[:, first:first + width], sh_a[:, first:first + width]
                dve.tensor_scalar(v, var, EPS, None, ALU.add).then_inc(var_ready, 1)
                if n == 1:
                    dve.wait_ge(setup_ps, 4)
                    link(dve.tensor_copy(vec[:, :], ps[:, 5, 0:ROWS]))
                bias, gamma, beta = (vec[:, r:r + width] for r in rows)
                link(dve.tensor_tensor(mu, mean, bias, ALU.add))
                link(dve.tensor_tensor(d, bias, mu, ALU.subtract))
                dve.wait_ge(root_ready, n + 1)
                link(dve.tensor_tensor(scale, root, gamma, ALU.mult))
                link(dve.tensor_tensor(d, d, scale, ALU.mult))
                dve.tensor_tensor(shift_, d, beta, ALU.add).then_inc(done, 1)

            row, col, diag, total, dinv = (deg[:, k, :] for k in range(5))
            dve.wait_ge(const_ready, 5)
            dve.wait_ge(ld_adj, 16)
            dve.reduce_sum(row, raw_a[:, :, :], axis=AX.X)
            for t in range(TT):
                block_ = slice(t * P, (t + 1) * P)
                last = dve.tensor_tensor(a_norm[:, t, block_], raw_a[:, t, block_], ident[:, :], ALU.mult)
            link(last)
            for t in range(TT):
                last = dve.reduce_sum(diag[:, t:t + 1], a_norm[:, t, t * P:(t + 1) * P], axis=AX.X)
            dve.wait_ge(setup_ps, 1)
            dve.tensor_copy(adj_t[:, :, :].rearrange("p t n -> p (t n)"), ps[:, 0, :]).then_inc(setup_sb, 1)
            dve.wait_ge(setup_sb, 1)
            link(dve.reduce_sum(col, adj_t[:, :, :], axis=AX.X))
            link(dve.scalar_tensor_tensor(out=total, in0=row, scalar=1.0, in1=col, op0=ALU.add, op1=ALU.add))
            dve.tensor_tensor(total, total, diag, ALU.subtract).then_inc(var_ready, 1)
            link(dve.tensor_copy(a_norm[:, :, :], raw_a[:, :, :]))
            for t in range(TT):
                block_ = slice(t * P, (t + 1) * P)
                last = dve.tensor_tensor(a_norm[:, t, block_], a_norm[:, t, block_], ident[:, :], ALU.add)
            link(last)
            dve.wait_ge(root_ready, 1)
            for t in range(TT):
                last = dve.tensor_scalar(a_norm[:, t, :], a_norm[:, t, :], dinv[:, t:t + 1], None, ALU.mult)
            last.then_inc(setup_sb, 1)
            dve.wait_ge(x_landed, 1)
            for k in range(2):
                row_stats(0, k)
            dve.wait_ge(setup_ps, 2)
            split(w1_hi[:, :, :], w1_lo[:, :, :], ps[:, 1, 0:HH * P].rearrange("p (k c) -> p k c", k=HH))
            dve.wait_ge(setup_ps, 3)
            for m in range(TT):
                last = dve.tensor_scalar(ahat_t[:, m, :], ps[:, 4, m * N:(m + 1) * N], dinv[:, m:m + 1], None, ALU.mult)
            last.then_inc(setup_sb, 1)

            def first_half(i, more):
                if more:
                    dve.wait_ge(x_landed, i + 2)
                for k in range(2):
                    dve.wait_ge(agg_head, 2 * i + k + 1)
                    dve.tensor_tensor(agg_lo[:, k, :], both(2 * k), agg_hi[:, k, :].bitcast(F32),
                                      ALU.subtract).then_inc(agg_tail, 1)
                for k in range(2):
                    if more:
                        row_stats(i + 1, k)
                    for hh in range(HH):
                        dve.wait_ge(z1_sb, 2 + 2 * (2 * i + k) + hh + 1)
                        for c in range(2):
                            dve.bn_stats(st1[:, hh, 2 * (2 * i + k) + c, :],
                                         z1[:, hh, 2 * i + k, c * BANK:(c + 1) * BANK]).then_inc(step, 1)

            with dve.Fori(0, CHUNKS - 1) as i:
                first_half(i, True)
            first_half(CHUNKS - 1, False)
            links["value"] = links["value"] + NG * HH * 2
            dve.wait_ge(step, links["value"])
            batchnorm_affine(1, [st1[:, hh, :, :] for hh in range(HH)], 0, HH, (R_B1, R_G1, R_BE1), bn1_ready)
            dve.wait_ge(setup_ps, 5)
            dve.tensor_copy(w2_t[:, :, :], ps[:, 6, 0:HH * P].rearrange("p (k c) -> p k c", k=HH)).then_inc(setup_sb, 1)
            dve.wait_ge(rs_ps, 1)
            split(rs_r[:, :], rs_l[:, :], ps[:, 7, 0:N]).then_inc(rs_read, 1)
            dve.wait_ge(rs_read, 1)
            dve.tensor_copy(rs_rows[0:1, :], rs_r[0:1, :].bitcast(F32))
            dve.tensor_copy(rs_rows[32:33, :], rs_l[32:33, :].bitcast(F32))
            dve.tensor_copy(rs_rows[64:65, :], rs_r[64:65, :].bitcast(F32))
            dve.wait_ge(ld_bg, 16 * 6)
            link(split(bg_r[:, :, :], bg_l[:, :, :], raw_bg[:, :, :]))
            dve.tensor_copy(bg_r[64:65, :, :], bg_l[64:65, :, :].bitcast(F32))
            dve.tensor_tensor(lbias[:, :], vec[:, R_BIH:R_BIH + SKIP * GATES], vec[:, R_BHH:R_BHH + SKIP * GATES], ALU.add)
            dve.tensor_copy(ident_r[:, :], ident[:, :])
            split(adj_hi[:, :, :], adj_lo[:, :, :], adj_t[:, :, :])
            dve.wait_ge(ld_w, 48)
            split(wg_hi[:, :, :], wg_lo[:, :, :], raw_g[:, :, :])

            def lstm_tail(n, bank):
                dve.wait_ge(wl_head, n + 1)
                dve.tensor_tensor(wl_lo[:, n, :, :].rearrange("p q c -> p (q c)"), bank,
                                  wl_hi[:, n, :, :].rearrange("p q c -> p (q c)").bitcast(F32),
                                  ALU.subtract).then_inc(wl_done, 1)

            with dve.Fori(0, CHUNKS) as i:
                for k in range(2):
                    dve.wait_ge(z2_ps, 2 * i + k + 1)
                    dve.tensor_copy(z2[:, 2 * i + k, :], both(4 + 2 * k)).then_inc(z2_sb, 1)
                    dve.wait_ge(z2_sb, 2 + 2 * i + k + 1)
                    for c in range(2):
                        dve.bn_stats(st2[:, 2 * (2 * i + k) + c, :],
                                     z2[:, 2 * i + k, c * BANK:(c + 1) * BANK]).then_inc(step, 1)
                    if k == 0:
                        lstm_tail(i, ps[:, i, :])
            links["value"] = links["value"] + NG * 2
            dve.wait_ge(step, links["value"])
            batchnorm_affine(2, [st2[:, :, :]], HH, 1, (R_B2, R_G2, R_BE2), bn2_ready)
            for n in range(4, NMAT):
                lstm_tail(n, ps[:, n % 4, :])

            def add_rows(i, k):
                dve.wait_ge(y_ps, 2 * i + k + 1)
                g4 = x_row[:, :, bass.ds(i * CB + k * GB, GB), :]
                dve.tensor_tensor(g4, ps[:, 4 + 2 * k:6 + 2 * k, :].rearrange("p t (b d) -> p t b d", b=GB), g4,
                                  ALU.add).then_inc(x1_ready, 1)

            def rows_tail(i, k):
                dve.wait_ge(n_head, 2 * i + k + 1)
                dve.tensor_tensor(s_lo[:, k, :], normed[:, k, :, :, :].rearrange("p t b d -> p (t b d)"),
                                  s_hi[:, k, :].bitcast(F32), ALU.subtract).then_inc(n_tail, 1)

            def graph_layers(i, more):
                for k in range(2):
                    dve.wait_ge(agg2_head, 2 * i + k + 1)
                    dve.tensor_tensor(s_lo[:, k, :], both(2 * k), s_hi[:, k, :].bitcast(F32),
                                      ALU.subtract).then_inc(agg2_tail, 1)
                for k in range(2):
                    if more:
                        add_rows(i + 1, k)
                        dve.wait_ge(x1_ready, 2 * i + 2 + k + 1)
                    dve.wait_ge(r_head, 2 * i + k + 1)
                    dve.scalar_tensor_tensor(out=r_lo[:, k, :], in0=both(2 * k), scalar=0.0,
                                             in1=r_hi[:, k, :].bitcast(F32), op0=ALU.max,
                                             op1=ALU.subtract).then_inc(r_tail, 1)
                    if more:
                        row_stats(i + 1, k)
                for k in range(2):
                    dve.wait_ge(u_head, 2 * i + k + 1)
                    dve.tensor_tensor(s_lo[:, k, :], both(4 + 2 * k), s_hi[:, k, :].bitcast(F32),
                                      ALU.subtract).then_inc(u_tail, 1)
                for k in range(2):
                    if more:
                        rows_tail(i + 1, k)
                    dve.wait_ge(h_head, 2 * i + k + 1)
                    head = h_hi[:, 2 * i + k, :].rearrange("p (t b) -> p t b", b=GB)
                    dve.scalar_tensor_tensor(out=h_lo[:, 2 * i + k, :].rearrange("p (t b) -> p t b", b=GB),
                                             in0=both(4 + 2 * k).rearrange("p (b t) -> p t b", b=GB), scalar=0.0,
                                             in1=head.bitcast(F32), op0=ALU.max, op1=ALU.subtract).then_inc(h_tail, 1)

            for k in range(2):
                add_rows(0, k)
                dve.wait_ge(x1_ready, k + 1)
                row_stats(0, k)
            for k in range(2):
                rows_tail(0, k)
            with dve.Fori(0, CHUNKS - 1) as i:
                graph_layers(i, True)
            graph_layers(CHUNKS - 1, False)

            PER_HALF = sum((3 if s else 2) for _, s, _, _ in STEPS) * HALF
            start = links["value"]
            with dve.Fori(0, 2) as half:
                links["value"] = half * PER_HALF + start

                def count(instruction):
                    links["value"] = links["value"] + 1
                    instruction.then_inc(step, 1)
                    return links["value"]

                def h_product(u, q, n):
                    _, _, _, windows = STEPS[n]
                    o_, tc_ = (gate[:, q, f, 0:windows * GB] for f in (3, 2))
                    dve.wait_ge(tc_ready, u + 1)
                    return count(dve.tensor_tensor(o_, o_, tc_, ALU.mult))

                def h_parts(q, n):
                    w, s, first, windows = STEPS[n]
                    h_ = gate[:, q, 3, 0:windows * GB]
                    if s < w - 1:
                        return mid_hi[:, q, 0:windows * GB], mid_lo[:, q, 0:windows * GB], h_
                    hi, lo = (seq(t, half * HALF + q, w, s, first, windows) for t in (h_hi, h_lo))
                    return hi, lo, h_.rearrange("p (t b) -> p t b", b=GB)

                before = None
                forgets = 0
                for n, (w, s, first, windows) in enumerate(STEPS):
                    cols = windows * GB
                    for q in range(HALF):
                        u = half * UNITS + (n * HALF + q)
                        i_, f_, g_ = (gate[:, q, f, 0:cols] for f in range(3))
                        c_ = cell[:, q, 0:cols]
                        if before:
                            h_there = h_product(*before)
                            hi, lo, h_ = h_parts(before[1], before[2])
                        dve.wait_ge(ig_ready, u + 1)
                        if s == 0:
                            dve.tensor_tensor(c_, i_, g_, ALU.mult).then_inc(c_ready, 1)
                        else:
                            dve.tensor_tensor(i_, i_, g_, ALU.mult)
                        if before:
                            dve.wait_ge(step, h_there)
                            head_there = count(dve.tensor_copy(hi, h_))
                        if s:
                            dve.wait_ge(f_ready, half * CARRIED + (forgets + 1))
                            forgets += 1
                            kept_there = count(dve.tensor_tensor(f_, f_, c_, ALU.mult))
                        if before:
                            dve.wait_ge(step, head_there)
                            dve.tensor_tensor(lo, h_, hi.bitcast(F32), ALU.subtract).then_inc(h_done, 1)
                        if s:
                            dve.wait_ge(step, kept_there)
                            dve.tensor_tensor(c_, i_, f_, ALU.add).then_inc(c_ready, 1)
                        before = (u, q, n)
                for q in range(HALF):
                    if q == 2:
                        h_there = h_product(*before)
                        hi, lo, h_ = h_parts(before[1], before[2])
                        dve.wait_ge(step, h_there)
                        head_there = count(dve.tensor_copy(hi, h_))
                        dve.wait_ge(step, head_there)
                        dve.tensor_tensor(lo, h_, hi.bitcast(F32), ALU.subtract).then_inc(h_done, 1)
                    g = half * HALF + q
                    dve.wait_ge(out_ps, g + 1)
                    dve.wait_ge(out_done[q % 2], half * (2 * 16 * TT) + (q // 2 + 1) * 16 * TT)
                    for t, bank in enumerate(((0, 1), (2, 3), (1, 5), (1, 5))[q]):
                        last = dve.tensor_tensor(o_row[:, q % 2, t, :, :], ps[:, bank, :].rearrange("p (b d) -> p b d", b=GB),
                                                 x_row[:, t, bass.ds(g * GB, GB), :], ALU.add)
                    last.then_inc(row_ready, 1)


_INS = ['x', 'adj', 'L0_gnn_W1', 'L0_gnn_b1', 'L0_gnn_g1', 'L0_gnn_be1', 'L0_gnn_W2', 'L0_gnn_b2', 'L0_gnn_g2',
        'L0_gnn_be2', 'L1_gnn_Wg0', 'L1_gnn_bg0', 'L1_gnn_Wg1', 'L1_gnn_bg1', 'L1_gnn_Wih', 'L1_gnn_Whh',
        'L1_gnn_bih', 'L1_gnn_bhh']


def kernel(**inputs):
    import numpy as _np
    import concourse.bacc as _bacc
    from concourse import mybir as _mybir
    from concourse.bass_utils import run_bass_kernel_spmd as _run

    nc = _bacc.Bacc("TRN2", target_bir_lowering=False, num_devices=1)
    arrays, args = {}, []
    for name in _INS:
        a = _np.ascontiguousarray(inputs[name])
        arrays[f"in_{name}_dram"] = a
        args.append(nc.dram_tensor(f"in_{name}_dram", a.shape, _mybir.dt.from_np(a.dtype), kind="ExternalInput").ap())
    shape = arrays["in_x_dram"].shape
    args.append(nc.dram_tensor("out_0_dram", shape, _mybir.dt.from_np(_np.dtype("float32")), kind="ExternalOutput").ap())
    gnn_lstm_kernel(nc, *args)
    r = _run(nc, [arrays], core_ids=[0])
    return r.results[0]["out_0_dram"]
```

```python
import concourse.bass as bass
from concourse import mybir
from contextlib import ExitStack

F32 = mybir.dt.float32
F32R = mybir.dt.float32r
ALU = mybir.AluOpType
ACT = mybir.ActivationFunctionType
AX = mybir.AxisListType

P = 128
KIB = 1024


def gnn_lstm_kernel(nc, x, adj, W1, b1, g1, be1, W2, b2, g2, be2,
                    Wg0, bg0, Wg1, bg1, Wih, Whh, bih, bhh, out):
    B, N, D = x.shape
    TT = N // P
    HH = W1.shape[0] // P
    GB = 4
    NG = B // GB
    GC = GB * N
    BANK = 512
    CHUNKS = NG // 2
    CB = 2 * GB
    SKIP = Wih.shape[0]
    GATES = Wih.shape[1] // P
    RG = TT * GB
    EPS = 1e-5
    R_B1, R_G1, R_BE1 = 0, HH, 2 * HH
    R_B2, R_G2, R_BE2 = 3 * HH, 3 * HH + 1, 3 * HH + 2
    R_BIH = 3 * HH + 3
    R_BHH = R_BIH + SKIP * GATES
    ROWS = R_BHH + SKIP * GATES

    ctx = ExitStack()
    with ctx:
        base = -(-nc.sbuf_base // 64) * 64

        def row_bytes(shape):
            n = 4
            for d in shape[1:]:
                n *= d
            return n

        def at(name, shape, dt, offset):
            return nc.alloc_sbuf_tensor_at(name, shape, dt, offset=base + offset)

        NMAT = 2 * SKIP - 1
        HALF = NG // 2
        AT_X, AT_Z, AT_Z2, AT_WL, AT_Y, AT_S, AT_R, AT_SMALL = (
            k * KIB for k in (0, 32, 96, 128, 156, 164, 180, 196))
        x_row = at("x_row", [P, TT, B, D], F32, AT_X)
        z1 = at("z1", [P, HH, NG, GC], F32, AT_Z)
        h_hi = at("h_hi", [P, NG, GC], F32R, AT_Z)
        h_lo = at("h_lo", [P, NG, GC], F32R, AT_Z + 32 * KIB)
        z2 = at("z2", [P, NG, GC], F32, AT_Z2)
        agg_hi = at("agg_hi", [P, 2, GC], F32R, AT_Z2)
        agg_lo = at("agg_lo", [P, 2, GC], F32R, AT_Z2 + 8 * KIB)
        ones = at("ones", [P, P], F32, AT_Z2 + 16 * KIB)
        rs_r = at("rs_r", [P, N], F32R, AT_Z2 + 17 * KIB)
        rs_l = at("rs_l", [P, N], F32R, AT_Z2 + 18 * KIB)
        bg_l = at("bg_l", [P, 2, P], F32R, AT_Z2 + 19 * KIB)
        ahat_hi = at("ahat_hi", [P, TT, N], F32R, AT_Z2 + 20 * KIB)
        ahat_lo = at("ahat_lo", [P, TT, N], F32R, AT_Z2 + 26 * KIB)
        raw_2 = at("raw_2", [P, HH * P], F32, AT_Z2 + 28 * KIB)
        raw_g = at("raw_g", [P, 2, D], F32, AT_Z2 + 29 * KIB)
        raw_bg = at("raw_bg", [P, 2, D], F32, AT_Z2 + 30 * KIB)
        raw_v = at("raw_v", [ROWS, D], F32, AT_Z2 + 31 * KIB)
        normed2 = at("normed2", [P, 2, TT, GB, D], F32, AT_Z2)
        w1_hi = at("w1_hi", [P, HH, P], F32R, AT_Z2 + 22 * KIB)
        w1_lo = at("w1_lo", [P, HH, P], F32R, AT_Z2 + 23 * KIB)
        adj_t = at("adj_t", [P, TT, N], F32, AT_Z2 + 24 * KIB)
        mid_hi = at("mid_hi", [P, HALF, BANK], F32R, AT_Z2)
        mid_lo = at("mid_lo", [P, HALF, BANK], F32R, AT_Z2 + 8 * KIB)
        cell = at("cell", [P, HALF, BANK], F32, AT_Z2 + 16 * KIB)
        h_sum = at("h_sum", [P, 2, GC], F32, AT_Z2 + 24 * KIB)
        wl_hi = at("wl_hi", [P, NMAT, GATES, P], F32R, AT_WL)
        wl_lo = at("wl_lo", [P, NMAT, GATES, P], F32R, AT_WL + NMAT * 2 * KIB)
        normed = at("normed", [P, 2, TT, GB, D], F32, AT_Y)
        y_col = at("y_col", [P, 2, GC], F32, AT_Y)
        s_hi = at("s_hi", [P, 2, GC], F32R, AT_S)
        s_lo = at("s_lo", [P, 2, GC], F32R, AT_S + 8 * KIB)
        r_hi = at("r_hi", [P, 2, GC], F32R, AT_R)
        r_lo = at("r_lo", [P, 2, GC], F32R, AT_R + 8 * KIB)
        gate = at("gate", [P, HALF, GATES, BANK], F32, AT_Y)
        st1 = at("st1", [P, HH, 2 * NG, 6], F32, AT_R + 15 * KIB)
        st2 = at("st2", [P, 2 * NG, 6], F32, AT_Y)
        w2_t = at("w2_t", [P, HH, P], F32, AT_R + 14 * KIB)
        raw_a = at("raw_a", [P, TT, N], F32, AT_Z + 48 * KIB)
        a_norm = at("a_norm", [P, TT, N], F32, AT_Z + 50 * KIB)
        raw_1 = at("raw_1", [P, HH, D], F32, AT_Z + 52 * KIB)
        ahat_t = at("ahat_t", [P, TT, N], F32, AT_Z + 54 * KIB)
        lnst1 = at("lnst1", [P, CHUNKS, 2 * RG, 6], F32, AT_Z + 60 * KIB)
        lnt1 = at("lnt1", [P, CHUNKS, 6, 2 * RG], F32, AT_Z + 62 * KIB)
        raw_l = at("raw_l", [P, NMAT, GATES, D], F32, AT_R)
        small = {"at": AT_SMALL}

        def sb(name, shape, dt=F32):
            t = at(name, shape, dt, small["at"])
            small["at"] += -(-row_bytes(shape) // 32) * 32
            return t

        ident = sb("ident", [P, P])
        adj_hi = sb("adj_hi", [P, TT, N], F32R)
        adj_lo = sb("adj_lo", [P, TT, N], F32R)
        wg_hi = sb("wg_hi", [P, 2, P], F32R)
        wg_lo = sb("wg_lo", [P, 2, P], F32R)
        bg_r = sb("bg_r", [P, 2, P], F32R)
        rs_rows = sb("rs_rows", [P, N], F32R)
        vec = sb("vec", [P, ROWS])
        lbias = sb("lbias", [P, SKIP * GATES])
        mv = sb("mv", [P, 3, 2])
        sc_a = sb("sc_a", [P, 3])
        sh_a = sb("sh_a", [P, 3])
        deg = sb("deg", [P, 5, TT])
        bnt = sb("bnt", [P, 4, HH])
        powers = sb("powers", [P, 2 * RG])
        lnst = sb("lnst", [P, 2, RG, 6])
        lnt = sb("lnt", [P, 2, 6, RG])
        rstd1 = sb("rstd1", [P, CHUNKS, 2 * RG])
        shift1 = sb("shift1", [P, CHUNKS, 2 * RG])
        rstd = sb("rstd", [P, 2, RG])
        shift = sb("shift", [P, 2, RG])
        ps = ctx.enter_context(nc.psum_tensor("ps", [P, 8, BANK], F32))

        def both(first):
            return ps[:, first:first + 2, :].rearrange("p a c -> p (a c)")

        def sem(name):
            return ctx.enter_context(nc.semaphore(name))

        ld_adj, ld_w1, ld_w, ld_vec, ld_bg, ld_lstm = (sem(n) for n in ("ld_adj", "ld_w1", "ld_w", "ld_vec", "ld_bg", "ld_lstm"))
        LOADS = [(0, GB), (GB, GB)] + [(c * CB, CB) for c in range(1, CHUNKS)]
        ld_x = [sem(f"ld_x{n}") for n in range(len(LOADS))]
        x_landed = sem("x_landed")
        const_ready = sem("const_ready")
        setup_ps = sem("setup_ps")
        setup_sb = sem("setup_sb")
        rs_ps = sem("rs_ps")
        rs_read = sem("rs_read")
        wl_ps, wl_head, wl_done = sem("wl_ps"), sem("wl_head"), sem("wl_done")
        step = sem("step")
        pstep = sem("pstep")
        var_ready, root_ready = sem("var_ready"), sem("root_ready")
        st_ready, stat_ready = sem("st_ready"), sem("stat_ready")
        n_act = sem("n_act")
        agg_ps, agg_head, agg_tail = (sem(n) for n in ("agg_ps", "agg_head", "agg_tail"))
        z1_ps, z1_sb = sem("z1_ps"), sem("z1_sb")
        bn1_ready, bn2_ready = sem("bn1_ready"), sem("bn2_ready")
        hid_ready = sem("hid_ready")
        z2_ps, z2_sb = sem("z2_ps"), sem("z2_sb")
        y_ready, y_ps, x1_ready = sem("y_ready"), sem("y_ps"), sem("x1_ready")
        n_ready, n_head, n_tail = sem("n_ready"), sem("n_head"), sem("n_tail")
        agg2_ps, agg2_head, agg2_tail = (sem(n) for n in ("agg2_ps", "agg2_head", "agg2_tail"))
        r_ps, r_head, r_tail = sem("r_ps"), sem("r_head"), sem("r_tail")
        u_ps, u_head, u_tail = sem("u_ps"), sem("u_head"), sem("u_tail")
        h_ps, h_head, h_tail = sem("h_ps"), sem("h_head"), sem("h_tail")
        gates_ps = sem("gates_ps")
        ig_ready, f_ready, o_ready = sem("ig_ready"), sem("f_ready"), sem("o_ready")
        c_ready, tc_ready, h_done = sem("c_ready"), sem("tc_ready"), sem("h_done")
        sum_ready, last_sum_ready = sem("sum_ready"), sem("last_sum_ready")
        out_ps, row_ready = sem("out_ps"), sem("row_ready")
        out_done = sem("out_done")

        def act_tiles(g):
            return RG // 2 if g < 2 else RG // 4

        LN_ROWS = [(first // CB, slice(first % CB // GB * RG, (first % CB + graphs) // GB * RG)) for first, graphs in LOADS]

        STEPS = []
        for w in range(1, SKIP + 1):
            count = N // w
            parts = -(-count * GB // BANK)
            for s in range(w):
                for c in range(parts):
                    STEPS.append((w, s, c * (count // parts), count // parts))
        LAST = len(STEPS) - 1
        ROWS_AFTER, ROWS_APART = 5, 2
        ORDER, due, units = [], [], 0
        for turn in range(NG // HALF):
            for n in range(len(STEPS)):
                for g in range(turn * HALF, (turn + 1) * HALF):
                    ORDER.append((g, n))
                    units += 1
                    if due and due[0][1] <= units:
                        ORDER.append((due.pop(0)[0], None))
                        due = [(g_, max(at_unit, units + ROWS_APART)) for g_, at_unit in due]
                    if n == LAST:
                        due.append((g, units + ROWS_AFTER))
        AT_END = [g for g, _ in due]
        ORDER += [(g, None) for g in AT_END]
        assert [g for g, n in ORDER if n is None] == list(range(NG))
        UNIT = {}
        for g, n in ORDER:
            if n is not None:
                UNIT[g, n] = len(UNIT)

        def row_banks(g):
            if g in AT_END:
                first = 2 * (AT_END.index(g) % 4)
                return first, first + 1
            return 1, 5

        LAST_G = NG - 1
        SUMS = 2

        def slot_done(g, n):
            if n:
                return UNIT[g, n - 1] + 1
            return UNIT[g - HALF, LAST] + 1 if g >= HALF else 0

        def seq(t, g, w, s, first, count):
            v = t[:, g, :].rearrange("p (t b) -> p t b", b=GB)
            lo = first * w + s
            return v[:, lo:lo + (count - 1) * w + 1:w, :]

        block = ctx.enter_context(nc.Block())

        @block.sync
        def _(sp):
            def load_x(n):
                first, graphs = LOADS[n]
                for t in range(TT):
                    sp.dma_start(x_row[:, t, first:first + graphs, :],
                                 x[first:first + graphs, t * P:(t + 1) * P, :].rearrange("b p d -> p b d")
                                 ).then_inc(ld_x[n], 16)

            sp.dma_start(raw_a[:, :, :], adj.rearrange("(t p) m -> p t m", p=P)).then_inc(ld_adj, 16)
            load_x(0)
            load_x(1)
            sp.dma_start(raw_1[:, :, :], W1.rearrange("(k p) d -> p k d", p=P)).then_inc(ld_w1, 16)
            for n in range(2, len(LOADS)):
                load_x(n)
            for n in range(len(LOADS)):
                sp.wait_ge(ld_x[n], 16 * TT)
                sp.sem_inc(x_landed, 1)
            sp.dma_start(raw_2[:, :], W2).then_inc(ld_w, 16)
            sp.dma_start(raw_g[:, 0, :], Wg0).then_inc(ld_w, 16)
            sp.dma_start(raw_g[:, 1, :], Wg1).then_inc(ld_w, 16)
            for w in range(SKIP):
                sp.dma_start(raw_l[:, w, :, :], Wih[w].rearrange("(q p) d -> p q d", p=P)).then_inc(ld_lstm, 16)
            for w in range(1, SKIP):
                sp.dma_start(raw_l[:, SKIP + w - 1, :, :], Whh[w].rearrange("(q p) d -> p q d", p=P)).then_inc(ld_lstm, 16)
            sp.wait_ge(const_ready, 5)
            for q in (0, 32, 64):
                for layer, v in ((0, bg0), (1, bg1)):
                    sp.dma_start(raw_bg[q:q + 1, layer, :], v.rearrange("(k p) -> k p", p=P)).then_inc(ld_bg, 16)
            with sp.Fori(0, NG) as g:
                for t in range(TT):
                    sp.wait_ge(row_ready, g * TT + (t + 1))
                    sp.dma_start(out[bass.ds(g * GB, GB), t * P:(t + 1) * P, :].rearrange("b p d -> p b d"),
                                 x_row[:, t, bass.ds(g * GB, GB), :]).then_inc(out_done, 16)
            sp.wait_ge(out_done, 16 * TT * NG)

        @block.gpsimd
        def _(pool):
            pool.memset(ident[:, :], 0.0).then_inc(const_ready, 1)
            pool.wait_ge(const_ready, 1)
            pool.affine_select(out=ident[:, :], in_=ident[:, :], compare_op=ALU.not_equal, fill=1.0,
                               base=0, pattern=[[-1, P]], channel_multiplier=1).then_inc(const_ready, 1)
            pool.memset(raw_bg[:, :, :], 0.0).then_inc(const_ready, 1)
            pool.memset(ones[:, :], 1.0).then_inc(const_ready, 1)
            pool.memset(rs_rows[:, :].bitcast(F32), 0.0).then_inc(const_ready, 1)
            pool.memset(powers[:, :], -0.5).then_inc(const_ready, 1)
            pool.wait_ge(const_ready, 6)

            links = {"value": 0}

            def link(instruction):
                links["value"] = links["value"] + 1
                instruction.then_inc(pstep, 1)
                pool.wait_ge(pstep, links["value"])

            def root(n, dst, v):
                pool.wait_ge(var_ready, n + 1)
                pool.tensor_tensor(dst, v, powers[:, 0:v.shape[-1]], ALU.pow).then_inc(root_ready, 1)

            def layernorm_stats(n, stats, temps, rstd_, shift_):
                even, odd = stats[:, :, 1], stats[:, :, 4]
                mean2, diff, both_, sq, v4, less_mean2 = temps
                half_r = both_
                pool.wait_ge(st_ready, n + 1)
                pool.tensor_tensor(mean2, even, odd, ALU.add)
                pool.tensor_tensor(diff, even, odd, ALU.subtract)
                link(pool.tensor_tensor(both_, stats[:, :, 2], stats[:, :, 5], ALU.add))
                pool.tensor_tensor(sq, diff, diff, ALU.mult)
                pool.tensor_scalar(less_mean2, mean2, -1.0, None, ALU.mult)
                link(pool.tensor_scalar(v4, both_, 4.0 / D, 4.0 * EPS, ALU.mult, ALU.add))
                link(pool.tensor_tensor(v4, v4, sq, ALU.add))
                link(pool.tensor_tensor(half_r, v4, powers[:, 0:v4.shape[-1]], ALU.pow))
                pool.tensor_tensor(shift_, less_mean2, half_r, ALU.mult)
                pool.tensor_scalar(rstd_, half_r, 2.0, None, ALU.mult).then_inc(stat_ready, 1)
                pool.wait_ge(stat_ready, n + 1)

            def normalise(dst, n, g, rstd_, shift_):
                k = g % 2
                if g >= 2:
                    pool.wait_ge(n_head, n - 1)
                    pool.wait_ge(n_tail, n - 1)
                for m in range(RG - act_tiles(g)):
                    t, b = divmod(m, GB)
                    last = pool.tensor_scalar(dst[:, k, t, b, :], x_row[:, t, g * GB + b, :],
                                              rstd_[:, m:m + 1], shift_[:, m:m + 1], ALU.mult, ALU.add)
                last.then_inc(n_ready, 1)

            root(0, deg[:, 4, :], deg[:, 3, :])
            for n, (first, graphs) in enumerate(LOADS):
                c, rows = LN_ROWS[n]
                layernorm_stats(n, lnst1[:, c, rows, :], [lnt1[:, c, t, rows] for t in range(6)],
                                rstd1[:, c, rows], shift1[:, c, rows])
                for g in range(first // GB, (first + graphs) // GB):
                    rows = slice(g % 2 * RG, (g % 2 + 1) * RG)
                    normalise(normed, g, g, rstd1[:, c, rows], shift1[:, c, rows])
            root(1, bnt[:, 1, 0:HH], bnt[:, 0, 0:HH])
            root(2, bnt[:, 1, 0:1], bnt[:, 0, 0:1])
            for g in range(NG):
                k = g % 2
                layernorm_stats(len(LOADS) + g, lnst[:, k, :, :], [lnt[:, k, t, :] for t in range(6)], rstd[:, k, :], shift[:, k, :])
                normalise(normed2, NG + g, g, rstd[:, k, :], shift[:, k, :])

            for g in range(LAST_G):
                pool.wait_ge(h_done, UNIT[g, LAST] + 1)
                if g >= SUMS:
                    pool.wait_ge(out_ps, g - SUMS + 1)
                pool.tensor_tensor(h_sum[:, g % SUMS, :], h_hi[:, g, :].bitcast(F32), h_lo[:, g, :].bitcast(F32),
                                   ALU.add).then_inc(sum_ready, 1)

        @block.tensor
        def _(pe):
            def three(dst, w_hi, w_lo, m_hi, m_lo, start, stop):
                pe.matmul(dst, w_hi, m_hi, start=start, stop=False, skip_group_check=True)
                pe.matmul(dst, w_hi, m_lo, start=False, stop=False, skip_group_check=True)
                return pe.matmul(dst, w_lo, m_hi, start=False, stop=stop, skip_group_check=True)

            def aggregate(k, a_hi, a_lo, done):
                for b in range(GB):
                    for m in range(TT):
                        rows = slice((m * GB + b) * D, (m * GB + b + 1) * D)
                        last = three(ps[:, 2 * k + b // 2, (b % 2) * N:(b % 2 + 1) * N], s_hi[:, k, rows], s_lo[:, k, rows],
                                     a_hi[:, m, :], a_lo[:, m, :], m == 0 and b % 2 == 0, m == TT - 1)
                last.then_inc(done, 1)

            pe.wait_ge(const_ready, 5)
            pe.wait_ge(ld_adj, 16)
            for m in range(TT):
                for n in range(TT):
                    last = pe.transpose(ps[:, 0, m * N + n * P:m * N + (n + 1) * P],
                                        raw_a[:, n, m * P:(m + 1) * P], ident[:, :])
            last.then_inc(setup_ps, 1)
            pe.wait_ge(ld_w1, 16)
            for k in range(HH):
                last = pe.transpose(ps[:, 1, k * P:(k + 1) * P], raw_1[:, k, :], ident[:, :])
            last.then_inc(setup_ps, 1)
            pe.wait_ge(setup_sb, 2)
            for m in range(TT):
                for n in range(TT):
                    last = pe.transpose(ps[:, 4, m * N + n * P:m * N + (n + 1) * P],
                                        a_norm[:, n, m * P:(m + 1) * P], ident[:, :])
            last.then_inc(setup_ps, 1)
            pe.wait_ge(setup_sb, 3)

            with pe.Fori(0, CHUNKS) as i:
                for k in range(2):
                    pe.wait_ge(n_tail, 2 * i + k + 1)
                    pe.wait_ge(agg_tail, 2 * i + k + 1)
                    aggregate(k, ahat_hi, ahat_lo, agg_ps)
                for k in range(2):
                    pe.wait_ge(agg_tail, 2 + 2 * i + k + 1)
                    for hh in range(HH):
                        pe.wait_ge(z1_sb, 2 * (2 * i + k) + hh + 1)
                        for c in range(2):
                            cols = slice(c * BANK, (c + 1) * BANK)
                            last = three(ps[:, 4 + 2 * hh + c, :], w1_hi[:, hh, :], w1_lo[:, hh, :],
                                         agg_hi[:, k, cols], agg_lo[:, k, cols], True, True)
                        last.then_inc(z1_ps, 1)

            pe.wait_ge(ld_vec, 16 * 8)
            pe.wait_ge(z1_sb, 2 + 2 * NG)
            pe.transpose(ps[:, 5, 0:ROWS], raw_v[:, :], ident[0:ROWS, 0:ROWS]).then_inc(setup_ps, 1)
            pe.wait_ge(ld_w, 48)
            for k in range(HH):
                last = pe.transpose(ps[:, 6, k * P:(k + 1) * P], raw_2[:, k * P:(k + 1) * P], ident[:, :])
            last.then_inc(setup_ps, 1)
            for m in range(TT):
                last = pe.matmul(ps[:, 7, 0:N], ones[:, :], adj_t[:, m, :], start=m == 0, stop=m == TT - 1)
            last.then_inc(rs_ps, 1)

            def transpose_lstm(first, count):
                for n in range(first, first + count):
                    for q in range(GATES):
                        last = pe.transpose(ps[:, n % 4, q * P:(q + 1) * P], raw_l[:, n, q, :], ident[:, :])
                    last.then_inc(wl_ps, 1)

            pe.wait_ge(ld_lstm, 16 * NMAT)
            transpose_lstm(0, 4)

            pe.wait_ge(setup_sb, 4)
            pe.wait_ge(rs_read, 1)
            with pe.Fori(0, CHUNKS) as i:
                for k in range(2):
                    pe.wait_ge(z2_sb, 2 * i + k + 1)
                    for hh in range(HH):
                        pe.wait_ge(hid_ready, HH * (2 * i + k) + hh + 1)
                        for c in range(2):
                            last = pe.matmul(ps[:, 4 + 2 * k + c, :], w2_t[:, hh, :],
                                             z1[:, hh, 2 * i + k, c * BANK:(c + 1) * BANK],
                                             start=hh == 0, stop=hh == HH - 1, skip_group_check=True)
                    last.then_inc(z2_ps, 1)
            pe.wait_ge(wl_done, 4)
            transpose_lstm(4, NMAT - 4)

            def rows_again(k, bank):
                for t in range(TT):
                    for b in range(GB):
                        last = pe.transpose(ps[:, bank + t, b * D:(b + 1) * D],
                                            y_col[:, k, b * N + t * P:b * N + (t + 1) * P], ident[:, :])
                last.then_inc(y_ps, 1)

            for n in range(4):
                pe.wait_ge(y_ready, n + 1)
                if n == 2:
                    pe.wait_ge(wl_done, NMAT)
                rows_again(n % 2, (4 + 2 * n) % 8)
            pe.wait_ge(x1_ready, 4)

            def graph_layers(i, rows_too):
                def rows_ahead(k):
                    if rows_too:
                        pe.wait_ge(y_ready, 2 * i + 4 + k + 1)
                        pe.wait_ge(h_tail, 2 * i + k + 1)
                        rows_again(k, 4 + 2 * k)

                for k in range(2):
                    pe.wait_ge(n_tail, NG + 2 * i + k + 1)
                    aggregate(k, adj_hi, adj_lo, agg2_ps)
                    if k == 0:
                        rows_ahead(0)
                for k in range(2):
                    pe.wait_ge(agg2_tail, 2 * i + k + 1)
                    for c in range(2):
                        dst = ps[:, 2 * k + c, :]
                        for n in range(2):
                            pe.matmul(dst[:, n * N:(n + 1) * N], bg_r[:, 0, :], rs_rows[:, :], start=n == 0, stop=False,
                                      skip_group_check=True)
                        cols = slice(c * BANK, (c + 1) * BANK)
                        last = three(dst, wg_hi[:, 0, :], wg_lo[:, 0, :], s_hi[:, k, cols], s_lo[:, k, cols], False, True)
                    last.then_inc(r_ps, 1)
                    if k == 0:
                        rows_ahead(1)
                for k in range(2):
                    pe.wait_ge(r_tail, 2 * i + k + 1)
                    if rows_too:
                        pe.wait_ge(x1_ready, 2 * i + 4 + k + 1)
                    else:
                        pe.wait_ge(h_tail, 2 * i + k + 1)
                    for n in range(GB * TT):
                        cols = slice(n * P, (n + 1) * P)
                        dst = ps[:, 4 + 2 * k + n // 4, (n % 4) * P:(n % 4 + 1) * P]
                        pe.matmul(dst, r_hi[:, k, cols], wg_hi[:, 1, :], start=True, stop=False, skip_group_check=True)
                        pe.matmul(dst, r_hi[:, k, cols], wg_lo[:, 1, :], start=False, stop=False, skip_group_check=True)
                        last = pe.matmul(dst, r_lo[:, k, cols], wg_hi[:, 1, :], start=False, stop=True, skip_group_check=True)
                    last.then_inc(u_ps, 1)
                for k in range(2):
                    pe.wait_ge(u_tail, 2 * i + k + 1)
                    for c in range(2):
                        for n in range(2):
                            pe.matmul(ps[:, 4 + 2 * k + c, n * N:(n + 1) * N], bg_r[:, 1, :], rs_rows[:, :],
                                      start=n == 0, stop=False, skip_group_check=True)
                    for b in range(GB):
                        for m in range(TT):
                            cols = slice(b * N + m * P, b * N + (m + 1) * P)
                            last = three(ps[:, 4 + 2 * k + b // 2, (b % 2) * N:(b % 2 + 1) * N],
                                         s_hi[:, k, cols], s_lo[:, k, cols],
                                         adj_hi[:, m, :], adj_lo[:, m, :], False, m == TT - 1)
                    last.then_inc(h_ps, 1)

            with pe.Fori(0, CHUNKS - 2) as i:
                graph_layers(i, True)
            for i in range(CHUNKS - 2, CHUNKS):
                graph_layers(i, False)

            def unit(k, g, n):
                w, s, first, count = STEPS[n]
                cols, q = count * GB, g % HALF
                x_hi, x_lo = (seq(t, g, w, s, first, count) for t in (h_hi, h_lo))
                gates = (0, 2, 1, 3) if s else (0, 2, 3)
                if s == 0 and w > 1:
                    pe.wait_ge(h_done, slot_done(g, n))
                for f in gates:
                    last = three(ps[:, 4 * k + f, 0:cols], wl_hi[:, w - 1, f, :], wl_lo[:, w - 1, f, :],
                                 x_hi, x_lo, True, s == 0)
                if s:
                    pe.wait_ge(h_done, slot_done(g, n))
                    m_hi, m_lo = mid_hi[:, q, 0:cols], mid_lo[:, q, 0:cols]
                    for f in gates:
                        last = three(ps[:, 4 * k + f, 0:cols], wl_hi[:, SKIP + w - 2, f, :],
                                     wl_lo[:, SKIP + w - 2, f, :], m_hi, m_lo, False, True)
                last.then_inc(gates_ps, 1)

            def rows_out(g):
                if g == LAST_G:
                    pe.wait_ge(last_sum_ready, 1)
                else:
                    pe.wait_ge(sum_ready, g + 1)
                v = h_sum[:, g % SUMS, :].rearrange("p (t b) -> p b t", b=GB)
                for t in range(TT):
                    for b in range(GB):
                        last = pe.transpose(ps[:, row_banks(g)[t], b * D:(b + 1) * D], v[:, b, t * P:(t + 1) * P], ident[:, :])
                last.then_inc(out_ps, 1)

            for g, n in ORDER:
                if n is None:
                    if g in AT_END:
                        pe.wait_ge(o_ready, len(UNIT) - 1 + AT_END.index(g) // 2)
                    else:
                        pe.wait_ge(o_ready, UNIT[g - g % HALF + HALF - 1, LAST] + 1)
                        if g:
                            pe.wait_ge(row_ready, TT * g)
                    rows_out(g)
                    continue
                u = UNIT[g, n]
                if u >= 2:
                    pe.wait_ge(o_ready, u - 1)
                else:
                    pe.wait_ge(h_tail, 2 + (NG if u else 1))
                if STEPS[n][1] and g >= HALF:
                    pe.wait_ge(row_ready, TT * (g - g % HALF))
                unit(u % 2, g, n)

        @block.scalar
        def _(act):
            act.sem_inc(z1_sb, 2)

            for row, v in ((R_B1, b1), (R_G1, g1), (R_BE1, be1)):
                act.dma_start(raw_v[row:row + HH, :], v.rearrange("(k p) -> k p", p=P)).then_inc(ld_vec, 16)
            for row, v in ((R_B2, b2), (R_G2, g2), (R_BE2, be2)):
                act.dma_start(raw_v[row:row + 1, :], v.rearrange("(k p) -> k p", p=P)).then_inc(ld_vec, 16)
            for row, v in ((R_BIH, bih), (R_BHH, bhh)):
                act.dma_start(raw_v[row:row + SKIP * GATES, :], v.rearrange("w (q p) -> (w q) p", p=P)).then_inc(ld_vec, 16)

            def normalise(dst, n, i, k, rstd_, shift_, tiles):
                for m in range(RG - tiles, RG):
                    t, b = divmod(m, GB)
                    last = act.activation(dst[:, k, t, b, :], x_row[:, t, i * CB + (k * GB + b), :], ACT.Identity,
                                          bias=shift_[:, m:m + 1], scale=rstd_[:, m:m + 1])
                last.then_inc(n_act, 1)
                act.wait_ge(n_act, n + 1)

            def normalise_1(i, k, tiles):
                n = 2 * i + k
                rows = slice(k * RG, (k + 1) * RG)
                normalise(normed, n, i, k, rstd1[:, i, rows], shift1[:, i, rows], tiles)

            def normalise_2(i, k, tiles):
                n = 2 * i + k
                act.wait_ge(stat_ready, len(LOADS) + n + 1)
                normalise(normed2, NG + n, i, k, rstd[:, k, :], shift[:, k, :], tiles)

            def rows_head(src, n, k):
                act.wait_ge(n_ready, n + 1)
                act.activation(s_hi[:, k, :], src[:, k, :, :, :].rearrange("p t b d -> p (t b d)"),
                               ACT.Relu).then_inc(n_head, 1)

            for k in range(2):
                act.wait_ge(stat_ready, k + 1)
                normalise_1(0, k, act_tiles(k))
                rows_head(normed, k, k)

            def first_half(i, more):
                def hidden(k, hh):
                    act.wait_ge(z1_ps, 2 * (2 * i + k) + hh + 1)
                    act.activation(z1[:, hh, 2 * i + k, :], both(4 + 2 * hh), ACT.Copy).then_inc(z1_sb, 1)

                def next_tiles(k):
                    act.wait_ge(stat_ready, i + 3)
                    act.wait_ge(n_tail, 2 * i + k + 1)
                    normalise_1(i + 1, k, act_tiles(2))

                for k in range(2):
                    act.wait_ge(agg_ps, 2 * i + k + 1)
                    act.activation(agg_hi[:, k, :], both(2 * k), ACT.Copy).then_inc(agg_head, 1)
                    if more and k == 0:
                        next_tiles(0)
                if more:
                    rows_head(normed, 2 * i + 2, 0)
                for hh in range(HH):
                    hidden(0, hh)
                if more:
                    next_tiles(1)
                    rows_head(normed, 2 * i + 3, 1)
                for hh in range(HH):
                    hidden(1, hh)

            with act.Fori(0, CHUNKS - 1) as i:
                first_half(i, True)
            first_half(CHUNKS - 1, False)

            def lstm_head(n, bank):
                act.wait_ge(wl_ps, n + 1)
                act.activation(wl_hi[:, n, :, :].rearrange("p q c -> p (q c)"), bank, ACT.Copy).then_inc(wl_head, 1)

            act.wait_ge(bn1_ready, 1)
            with act.Fori(0, CHUNKS) as i:
                for k in range(2):
                    for hh in range(HH):
                        v = z1[:, hh, 2 * i + k, :]
                        act.activation(v, v, ACT.Relu, bias=sh_a[:, hh:hh + 1],
                                       scale=sc_a[:, hh:hh + 1]).then_inc(hid_ready, 1)
                lstm_head(i, ps[:, i, :])
            for n in range(4, NMAT):
                lstm_head(n, ps[:, n % 4, :])
            act.wait_ge(bn2_ready, 1)

            def batchnormed(i, k):
                if i:
                    act.wait_ge(y_ps, 2 * i + k - 1)
                act.activation(y_col[:, k, :], z2[:, 2 * i + k, :], ACT.Identity,
                               bias=sh_a[:, 2:3], scale=sc_a[:, 2:3]).then_inc(y_ready, 1)

            def graph_layers(i, more, batch_too):
                for k in range(2):
                    act.wait_ge(agg2_ps, 2 * i + k + 1)
                    act.activation(s_hi[:, k, :], both(2 * k), ACT.Copy).then_inc(agg2_head, 1)
                for k in range(2):
                    act.wait_ge(r_ps, 2 * i + k + 1)
                    act.activation(r_hi[:, k, :], both(2 * k), ACT.Relu).then_inc(r_head, 1)
                for k in range(2):
                    act.wait_ge(u_ps, 2 * i + k + 1)
                    act.activation(s_hi[:, k, :], both(4 + 2 * k), ACT.Copy).then_inc(u_head, 1)
                    if batch_too and k == 0:
                        batchnormed(i + 3, 0)
                for k in range(2):
                    if more:
                        normalise_2(i + 1, k, act_tiles(2))
                    if batch_too and k == 0:
                        batchnormed(i + 3, 1)
                    act.wait_ge(h_ps, 2 * i + k + 1)
                    if more:
                        rows_head(normed2, NG + 2 * i + 2 + k, k)
                    act.activation(h_hi[:, 2 * i + k, :].rearrange("p (t b) -> p t b", b=GB),
                                   both(4 + 2 * k).rearrange("p (b t) -> p t b", b=GB), ACT.Relu).then_inc(h_head, 1)

            for i in range(2):
                for k in range(2):
                    batchnormed(i, k)
            for k in range(2):
                normalise_2(0, k, act_tiles(k))
                rows_head(normed2, NG + k, k)
            for k in range(2):
                batchnormed(2, k)
            for i in range(CHUNKS):
                graph_layers(i, i + 1 < CHUNKS, i + 3 < CHUNKS)

            def tanh_c(u, q, cols):
                act.wait_ge(c_ready, u + 1)
                act.activation(gate[:, q, 2, 0:cols], cell[:, q, 0:cols], ACT.Tanh).then_inc(tc_ready, 1)

            before = None
            for g, n in ORDER:
                if n is None:
                    continue
                w, s, first, count = STEPS[n]
                cols, q, u = count * GB, g % HALF, UNIT[g, n]
                if before and slot_done(g, n) == u:
                    tanh_c(*before)
                    before = None
                for f in (0, 2, 1, 3) if s else (0, 2, 3):
                    if f == 0:
                        act.wait_ge(gates_ps, u + 1)
                        if slot_done(g, n):
                            act.wait_ge(h_done, slot_done(g, n))
                    col = (w - 1) * GATES + f
                    last = act.activation(gate[:, q, f, 0:cols], ps[:, 4 * (u % 2) + f, 0:cols],
                                          ACT.Tanh if f == 2 else ACT.Sigmoid, bias=lbias[:, col:col + 1])
                    if f == 2:
                        last.then_inc(ig_ready, 1)
                        if before:
                            tanh_c(*before)
                    elif f == 1:
                        last.then_inc(f_ready, 1)
                last.then_inc(o_ready, 1)
                before = (u, q, cols)
            tanh_c(*before)

        @block.vector
        def _(dve):
            for s in (agg_tail, z2_sb, h_tail):
                dve.sem_inc(s, 2)
            links = {"value": 0}

            def link(instruction):
                links["value"] = links["value"] + 1
                instruction.then_inc(step, 1)
                dve.wait_ge(step, links["value"])

            def split(head, tail, src):
                link(dve.tensor_copy(head, src))
                return dve.tensor_tensor(tail, src, head.bitcast(F32), ALU.subtract)

            def rows_tail(src, n, k):
                dve.wait_ge(n_head, n + 1)
                dve.scalar_tensor_tensor(out=s_lo[:, k, :], in0=src[:, k, :, :, :].rearrange("p t b d -> p (t b d)"),
                                         scalar=0.0, in1=s_hi[:, k, :].bitcast(F32), op0=ALU.max,
                                         op1=ALU.subtract).then_inc(n_tail, 1)

            def row_stats(i, k):
                for t in range(TT):
                    for b in range(GB):
                        last = dve.bn_stats(lnst[:, k, t * GB + b, :], x_row[:, t, i * CB + (k * GB + b), :])
                last.then_inc(st_ready, 1)

            def batchnorm_affine(n, stats, first, width, rows, done):
                for k, s in enumerate(stats):
                    last = dve.bn_aggr(mv[:, first + k, :], s)
                link(last)
                mean, var = mv[:, first:first + width, 0], mv[:, first:first + width, 1]
                v, root, mu, d = (bnt[:, t, 0:width] for t in range(4))
                scale, shift_ = sc_a[:, first:first + width], sh_a[:, first:first + width]
                dve.tensor_scalar(v, var, EPS, None, ALU.add).then_inc(var_ready, 1)
                if n == 1:
                    dve.wait_ge(setup_ps, 4)
                    link(dve.tensor_copy(vec[:, :], ps[:, 5, 0:ROWS]))
                bias, gamma, beta = (vec[:, r:r + width] for r in rows)
                link(dve.tensor_tensor(mu, mean, bias, ALU.add))
                link(dve.tensor_tensor(d, bias, mu, ALU.subtract))
                dve.wait_ge(root_ready, n + 1)
                link(dve.tensor_tensor(scale, root, gamma, ALU.mult))
                link(dve.tensor_tensor(d, d, scale, ALU.mult))
                dve.tensor_tensor(shift_, d, beta, ALU.add).then_inc(done, 1)

            row, col, diag, total, dinv = (deg[:, k, :] for k in range(5))
            dve.wait_ge(const_ready, 5)
            dve.wait_ge(ld_adj, 16)
            dve.reduce_sum(row, raw_a[:, :, :], axis=AX.X)
            for t in range(TT):
                block_ = slice(t * P, (t + 1) * P)
                last = dve.tensor_tensor(a_norm[:, t, block_], raw_a[:, t, block_], ident[:, :], ALU.mult)
            link(last)
            for t in range(TT):
                last = dve.reduce_sum(diag[:, t:t + 1], a_norm[:, t, t * P:(t + 1) * P], axis=AX.X)
            dve.wait_ge(setup_ps, 1)
            dve.tensor_copy(adj_t[:, :, :].rearrange("p t n -> p (t n)"), ps[:, 0, :]).then_inc(setup_sb, 1)
            dve.wait_ge(setup_sb, 1)
            link(dve.reduce_sum(col, adj_t[:, :, :], axis=AX.X))
            link(dve.scalar_tensor_tensor(out=total, in0=row, scalar=1.0, in1=col, op0=ALU.add, op1=ALU.add))
            dve.tensor_tensor(total, total, diag, ALU.subtract).then_inc(var_ready, 1)
            link(dve.tensor_copy(a_norm[:, :, :], raw_a[:, :, :]))
            for t in range(TT):
                block_ = slice(t * P, (t + 1) * P)
                last = dve.tensor_tensor(a_norm[:, t, block_], a_norm[:, t, block_], ident[:, :], ALU.add)
            link(last)
            dve.wait_ge(root_ready, 1)
            for t in range(TT):
                last = dve.tensor_scalar(a_norm[:, t, :], a_norm[:, t, :], dinv[:, t:t + 1], None, ALU.mult)
            last.then_inc(setup_sb, 1)

            def load_stats(n, c, first, graphs):
                dve.wait_ge(x_landed, n)
                for b in range(first, first + graphs):
                    for t in range(TT):
                        m = (b // GB * TT + t) * GB + b % GB
                        last = dve.bn_stats(lnst1[:, c, m, :], x_row[:, t, c * CB + b, :])
                return last

            load_stats(1, 0, 0, GB).then_inc(st_ready, 1)
            load_stats(2, 0, GB, GB).then_inc(st_ready, 1)
            dve.wait_ge(setup_ps, 2)
            split(w1_hi[:, :, :], w1_lo[:, :, :], ps[:, 1, 0:HH * P].rearrange("p (k c) -> p k c", k=HH))
            dve.wait_ge(setup_ps, 3)
            for m in range(TT):
                last = dve.tensor_scalar(ahat_t[:, m, :], ps[:, 4, m * N:(m + 1) * N], dinv[:, m:m + 1], None, ALU.mult)
            link(last)
            split(ahat_hi[:, :, :], ahat_lo[:, :, :], ahat_t[:, :, :]).then_inc(setup_sb, 1)
            rows_tail(normed, 0, 0)
            load_stats(3, 1, 0, CB).then_inc(st_ready, 1)
            rows_tail(normed, 1, 1)
            load_stats(4, 2, 0, CB).then_inc(st_ready, 1)

            def first_half(i, more, stats_too):
                def hidden_stats(k, hh):
                    dve.wait_ge(z1_sb, 2 + 2 * (2 * i + k) + hh + 1)
                    for c in range(2):
                        dve.bn_stats(st1[:, hh, 2 * (2 * i + k) + c, :],
                                     z1[:, hh, 2 * i + k, c * BANK:(c + 1) * BANK]).then_inc(step, 1)

                for k in range(2):
                    dve.wait_ge(agg_head, 2 * i + k + 1)
                    dve.tensor_tensor(agg_lo[:, k, :], both(2 * k), agg_hi[:, k, :].bitcast(F32),
                                      ALU.subtract).then_inc(agg_tail, 1)
                if stats_too:
                    load_stats(len(LOADS), CHUNKS - 1, 0, CB).then_inc(st_ready, 1)
                if more:
                    rows_tail(normed, 2 * i + 2, 0)
                for hh in range(HH):
                    hidden_stats(0, hh)
                if more:
                    rows_tail(normed, 2 * i + 3, 1)
                for hh in range(HH):
                    hidden_stats(1, hh)

            first_half(0, True, True)
            with dve.Fori(1, CHUNKS - 1) as i:
                first_half(i, True, False)
            first_half(CHUNKS - 1, False, False)
            links["value"] = links["value"] + NG * HH * 2
            dve.wait_ge(step, links["value"])
            batchnorm_affine(1, [st1[:, hh, :, :] for hh in range(HH)], 0, HH, (R_B1, R_G1, R_BE1), bn1_ready)
            dve.wait_ge(setup_ps, 5)
            dve.tensor_copy(w2_t[:, :, :], ps[:, 6, 0:HH * P].rearrange("p (k c) -> p k c", k=HH)).then_inc(setup_sb, 1)
            dve.wait_ge(rs_ps, 1)
            split(rs_r[:, :], rs_l[:, :], ps[:, 7, 0:N]).then_inc(rs_read, 1)
            dve.wait_ge(rs_read, 1)
            dve.tensor_copy(rs_rows[0:1, :], rs_r[0:1, :].bitcast(F32))
            dve.tensor_copy(rs_rows[32:33, :], rs_l[32:33, :].bitcast(F32))
            dve.tensor_copy(rs_rows[64:65, :], rs_r[64:65, :].bitcast(F32))
            dve.wait_ge(ld_bg, 16 * 6)
            link(split(bg_r[:, :, :], bg_l[:, :, :], raw_bg[:, :, :]))
            dve.tensor_copy(bg_r[64:65, :, :], bg_l[64:65, :, :].bitcast(F32))
            dve.tensor_tensor(lbias[:, :], vec[:, R_BIH:R_BIH + SKIP * GATES], vec[:, R_BHH:R_BHH + SKIP * GATES], ALU.add)
            split(adj_hi[:, :, :], adj_lo[:, :, :], adj_t[:, :, :])
            dve.wait_ge(ld_w, 48)
            split(wg_hi[:, :, :], wg_lo[:, :, :], raw_g[:, :, :])

            def lstm_tail(n, bank):
                dve.wait_ge(wl_head, n + 1)
                dve.tensor_tensor(wl_lo[:, n, :, :].rearrange("p q c -> p (q c)"), bank,
                                  wl_hi[:, n, :, :].rearrange("p q c -> p (q c)").bitcast(F32),
                                  ALU.subtract).then_inc(wl_done, 1)

            with dve.Fori(0, CHUNKS) as i:
                for k in range(2):
                    dve.wait_ge(z2_ps, 2 * i + k + 1)
                    dve.tensor_copy(z2[:, 2 * i + k, :], both(4 + 2 * k)).then_inc(z2_sb, 1)
                    dve.wait_ge(z2_sb, 2 + 2 * i + k + 1)
                    for c in range(2):
                        dve.bn_stats(st2[:, 2 * (2 * i + k) + c, :],
                                     z2[:, 2 * i + k, c * BANK:(c + 1) * BANK]).then_inc(step, 1)
                    if k == 0:
                        lstm_tail(i, ps[:, i, :])
            links["value"] = links["value"] + NG * 2
            dve.wait_ge(step, links["value"])
            batchnorm_affine(2, [st2[:, :, :]], HH, 1, (R_B2, R_G2, R_BE2), bn2_ready)
            for n in range(4, NMAT):
                lstm_tail(n, ps[:, n % 4, :])

            def add_rows(i, k, bank):
                dve.wait_ge(y_ps, 2 * i + k + 1)
                g4 = x_row[:, :, bass.ds(i * CB + k * GB, GB), :]
                dve.tensor_tensor(g4, ps[:, bank:bank + 2, :].rearrange("p t (b d) -> p t b d", b=GB), g4,
                                  ALU.add).then_inc(x1_ready, 1)

            def graph_layers(i, more, rows_too):
                for k in range(2):
                    dve.wait_ge(agg2_head, 2 * i + k + 1)
                    dve.tensor_tensor(s_lo[:, k, :], both(2 * k), s_hi[:, k, :].bitcast(F32),
                                      ALU.subtract).then_inc(agg2_tail, 1)
                    if more and k == 0:
                        row_stats(i + 1, 0)
                if rows_too:
                    add_rows(i + 2, 0, 4)
                for k in range(2):
                    dve.wait_ge(r_head, 2 * i + k + 1)
                    dve.scalar_tensor_tensor(out=r_lo[:, k, :], in0=both(2 * k), scalar=0.0,
                                             in1=r_hi[:, k, :].bitcast(F32), op0=ALU.max,
                                             op1=ALU.subtract).then_inc(r_tail, 1)
                    if rows_too and k == 0:
                        add_rows(i + 2, 1, 6)
                if more:
                    row_stats(i + 1, 1)
                for k in range(2):
                    dve.wait_ge(u_head, 2 * i + k + 1)
                    dve.tensor_tensor(s_lo[:, k, :], both(4 + 2 * k), s_hi[:, k, :].bitcast(F32),
                                      ALU.subtract).then_inc(u_tail, 1)
                for k in range(2):
                    if more:
                        rows_tail(normed2, NG + 2 * i + 2 + k, k)
                    dve.wait_ge(h_head, 2 * i + k + 1)
                    head = h_hi[:, 2 * i + k, :].rearrange("p (t b) -> p t b", b=GB)
                    dve.scalar_tensor_tensor(out=h_lo[:, 2 * i + k, :].rearrange("p (t b) -> p t b", b=GB),
                                             in0=both(4 + 2 * k).rearrange("p (b t) -> p t b", b=GB), scalar=0.0,
                                             in1=head.bitcast(F32), op0=ALU.max, op1=ALU.subtract).then_inc(h_tail, 1)

            for k in range(2):
                add_rows(0, k, 4 + 2 * k)
                dve.wait_ge(x1_ready, k + 1)
                row_stats(0, k)
            for k in range(2):
                add_rows(1, k, 2 * k)
            dve.wait_ge(x1_ready, 4)
            for k in range(2):
                rows_tail(normed2, NG + k, k)
            with dve.Fori(0, CHUNKS - 2) as i:
                graph_layers(i, True, True)
            graph_layers(CHUNKS - 2, True, False)
            graph_layers(CHUNKS - 1, False, False)

            def count(instruction):
                links["value"] = links["value"] + 1
                instruction.then_inc(step, 1)
                return links["value"]

            def h_product(g, n):
                o_, tc_ = (gate[:, g % HALF, f, 0:STEPS[n][3] * GB] for f in (3, 2))
                dve.wait_ge(tc_ready, UNIT[g, n] + 1)
                return count(dve.tensor_tensor(o_, o_, tc_, ALU.mult))

            def h_parts(g, n):
                w, s, first, windows = STEPS[n]
                q = g % HALF
                h_ = gate[:, q, 3, 0:windows * GB]
                if s < w - 1:
                    return mid_hi[:, q, 0:windows * GB], mid_lo[:, q, 0:windows * GB], h_
                hi, lo = (seq(t, g, w, s, first, windows) for t in (h_hi, h_lo))
                return hi, lo, h_.rearrange("p (t b) -> p t b", b=GB)

            def finish(g, n):
                h_there = h_product(g, n)
                hi, lo, h_ = h_parts(g, n)
                dve.wait_ge(step, h_there)
                head_there = count(dve.tensor_copy(hi, h_))
                dve.wait_ge(step, head_there)
                dve.tensor_tensor(lo, h_, hi.bitcast(F32), ALU.subtract).then_inc(h_done, 1)

            def add_result(g):
                dve.wait_ge(out_ps, g + 1)
                for t, bank in enumerate(row_banks(g)):
                    rows = x_row[:, t, g * GB:(g + 1) * GB, :]
                    dve.tensor_tensor(rows, ps[:, bank, :].rearrange("p (b d) -> p b d", b=GB), rows,
                                      ALU.add).then_inc(row_ready, 1)

            before = None
            forgets = 0
            for g, n in ORDER:
                if n is None:
                    if before and g in AT_END:
                        finish(*before)
                        before = None
                        dve.wait_ge(h_done, UNIT[LAST_G, LAST] + 1)
                        dve.wait_ge(out_ps, LAST_G - SUMS + 1)
                        dve.tensor_tensor(h_sum[:, LAST_G % SUMS, :], h_hi[:, LAST_G, :].bitcast(F32),
                                          h_lo[:, LAST_G, :].bitcast(F32), ALU.add).then_inc(last_sum_ready, 1)
                    add_result(g)
                    continue
                w, s, first, windows = STEPS[n]
                q, cols, u = g % HALF, windows * GB, UNIT[g, n]
                if before and slot_done(g, n) == u:
                    finish(*before)
                    before = None
                i_, f_, g_ = (gate[:, q, f, 0:cols] for f in range(3))
                c_ = cell[:, q, 0:cols]
                dve.wait_ge(ig_ready, u + 1)
                if s == 0:
                    dve.tensor_tensor(c_, i_, g_, ALU.mult).then_inc(c_ready, 1)
                else:
                    dve.tensor_tensor(i_, i_, g_, ALU.mult)
                if before:
                    h_there = h_product(*before)
                    hi, lo, h_ = h_parts(*before)
                if s:
                    forgets += 1
                    dve.wait_ge(f_ready, forgets)
                    kept_there = count(dve.tensor_tensor(f_, f_, c_, ALU.mult))
                if before:
                    dve.wait_ge(step, h_there)
                    head_there = count(dve.tensor_copy(hi, h_))
                if s:
                    dve.wait_ge(step, kept_there)
                    dve.tensor_tensor(c_, i_, f_, ALU.add).then_inc(c_ready, 1)
                if before:
                    dve.wait_ge(step, head_there)
                    dve.tensor_tensor(lo, h_, hi.bitcast(F32), ALU.subtract).then_inc(h_done, 1)
                before = (g, n)
            if before:
                finish(*before)


_INS = ['x', 'adj', 'L0_gnn_W1', 'L0_gnn_b1', 'L0_gnn_g1', 'L0_gnn_be1', 'L0_gnn_W2', 'L0_gnn_b2', 'L0_gnn_g2',
        'L0_gnn_be2', 'L1_gnn_Wg0', 'L1_gnn_bg0', 'L1_gnn_Wg1', 'L1_gnn_bg1', 'L1_gnn_Wih', 'L1_gnn_Whh',
        'L1_gnn_bih', 'L1_gnn_bhh']


def kernel(**inputs):
    import numpy as _np
    import concourse.bacc as _bacc
    from concourse import mybir as _mybir
    from concourse.bass_utils import run_bass_kernel_spmd as _run

    nc = _bacc.Bacc("TRN2", target_bir_lowering=False, num_devices=1)
    arrays, args = {}, []
    for name in _INS:
        a = _np.ascontiguousarray(inputs[name])
        arrays[f"in_{name}_dram"] = a
        args.append(nc.dram_tensor(f"in_{name}_dram", a.shape, _mybir.dt.from_np(a.dtype), kind="ExternalInput").ap())
    shape = arrays["in_x_dram"].shape
    args.append(nc.dram_tensor("out_0_dram", shape, _mybir.dt.from_np(_np.dtype("float32")), kind="ExternalOutput").ap())
    gnn_lstm_kernel(nc, *args)
    r = _run(nc, [arrays], core_ids=[0])
    return r.results[0]["out_0_dram"]
```
